# Optimizing a Trainium2 kernel written in Bass

```python
import numpy as np
import jax
import jax.numpy as jnp

def _softmax(x, axis=-1):
    return jax.nn.softmax(x, axis=axis)

def _gelu(x):
    return jax.nn.gelu(x, approximate=True)

def _silu(x):
    return jax.nn.silu(x)

def _sigmoid(x):
    return jax.nn.sigmoid(x)

def _layernorm(x, axis=-1, eps=1e-05):
    m = jnp.mean(x, axis=axis, keepdims=True)
    v = jnp.var(x, axis=axis, keepdims=True)
    return (x - m) / jnp.sqrt(v + eps)

def _scatter_add(tgt, idx, src, axis=0):
    return tgt.at[idx].add(src)

def _segment_sum(src, seg, n):
    return jax.ops.segment_sum(src, seg, n)
kernel_name = 'mk_macaron_d1_jaxref_r4_16e051'

def setup_inputs(seed: int=0):
    np.random.seed(seed)
    _w = jnp.asarray

    def _L0_attn_setup():
        import jax, jax.numpy as jnp
        import numpy as np
        D_MODEL = 256
        IDX_HEADS = 4
        IDX_DIM = 64
        TOP_K = 64

        def _rope(x):
            B, S, D = x.shape
            half = D // 2
            inv_freq = 1.0 / 10000.0 ** (jnp.arange(half, dtype=jnp.float32) / half)
            ang = jnp.arange(S, dtype=jnp.float32)[:, None] * inv_freq[None, :]
            cos, sin = (jnp.cos(ang), jnp.sin(ang))
            x1, x2 = (x[..., :half], x[..., half:])
            return jnp.concatenate([x1 * cos - x2 * sin, x1 * sin + x2 * cos], axis=-1)
        key = jax.random.key(seed)
        ks = jax.random.split(key, 11)
        B, S, D = (2, 1024, D_MODEL)
        s = 0.02
        return {'x': jax.random.normal(ks[0], (B, S, D), dtype=jnp.float32), 'w_qkv': jax.random.normal(ks[1], (3 * D, D), dtype=jnp.float32) * s, 'b_qkv': jnp.zeros((3 * D,), dtype=jnp.float32), 'w_o': jax.random.normal(ks[2], (D, D), dtype=jnp.float32) * s, 'b_o': jnp.zeros((D,), dtype=jnp.float32), 'w_iq': jax.random.normal(ks[3], (IDX_HEADS * IDX_DIM, D), dtype=jnp.float32) * s, 'b_iq': jnp.zeros((IDX_HEADS * IDX_DIM,), dtype=jnp.float32), 'w_ik': jax.random.normal(ks[4], (IDX_DIM, D), dtype=jnp.float32) * s, 'b_ik': jnp.zeros((IDX_DIM,), dtype=jnp.float32), 'w_iw': jax.random.normal(ks[5], (IDX_HEADS, D), dtype=jnp.float32) * s, 'b_iw': jnp.zeros((IDX_HEADS,), dtype=jnp.float32)}
    _L0_attn_in = _L0_attn_setup()

    def _L0_ffn_setup():
        import jax, jax.numpy as jnp
        import numpy as np
        E = 8
        key = jax.random.key(seed)
        k0, k1, k2, k3 = jax.random.split(key, 4)
        B, S, H, F = (4, 1024, 256, 1024)
        x = jax.random.normal(k0, (B, S, H), jnp.float32)
        Wr = jax.random.normal(k1, (E, H), jnp.float32) * 0.02
        W1 = jax.random.normal(k2, (E, H, F), jnp.float32) * 0.02
        b1 = jnp.zeros((E, F), jnp.float32)
        W2 = jax.random.normal(k3, (E, F, H), jnp.float32) * 0.02
        b2 = jnp.zeros((E, H), jnp.float32)
        return {'x': x, 'Wr': Wr, 'W1': W1, 'b1': b1, 'W2': W2, 'b2': b2}
    _L0_ffn_in = _L0_ffn_setup()
    _d = {'L0_attn_x': _L0_attn_in['x'], 'L0_attn_w_qkv': _L0_attn_in['w_qkv'], 'L0_attn_b_qkv': _L0_attn_in['b_qkv'], 'L0_attn_w_o': _L0_attn_in['w_o'], 'L0_attn_b_o': _L0_attn_in['b_o'], 'L0_attn_w_iq': _L0_attn_in['w_iq'], 'L0_attn_b_iq': _L0_attn_in['b_iq'], 'L0_attn_w_ik': _L0_attn_in['w_ik'], 'L0_attn_b_ik': _L0_attn_in['b_ik'], 'L0_attn_w_iw': _L0_attn_in['w_iw'], 'L0_attn_b_iw': _L0_attn_in['b_iw'], 'L0_ffn_Wr': _L0_ffn_in['Wr'], 'L0_ffn_W1': _L0_ffn_in['W1'], 'L0_ffn_b1': _L0_ffn_in['b1'], 'L0_ffn_W2': _L0_ffn_in['W2'], 'L0_ffn_b2': _L0_ffn_in['b2']}
    _x0 = _d['L0_attn_x']
    _d['L0_attn_x'] = jax.random.normal(jax.random.fold_in(jax.random.key(seed), 1), (4, 2048, 256), dtype=_x0.dtype)
    del _x0
    return _d

def reference(L0_attn_x, L0_attn_w_qkv, L0_attn_b_qkv, L0_attn_w_o, L0_attn_b_o, L0_attn_w_iq, L0_attn_b_iq, L0_attn_w_ik, L0_attn_b_ik, L0_attn_w_iw, L0_attn_b_iw, L0_ffn_Wr, L0_ffn_W1, L0_ffn_b1, L0_ffn_W2, L0_ffn_b2):

    def _L0_attn_ref(x, w_qkv, b_qkv, w_o, b_o, w_iq, b_iq, w_ik, b_ik, w_iw, b_iw):
        import jax, jax.numpy as jnp
        import numpy as np
        D_MODEL = 256
        IDX_HEADS = 4
        IDX_DIM = 64
        TOP_K = 64

        def _rope(x):
            B, S, D = x.shape
            half = D // 2
            inv_freq = 1.0 / 10000.0 ** (jnp.arange(half, dtype=jnp.float32) / half)
            ang = jnp.arange(S, dtype=jnp.float32)[:, None] * inv_freq[None, :]
            cos, sin = (jnp.cos(ang), jnp.sin(ang))
            x1, x2 = (x[..., :half], x[..., half:])
            return jnp.concatenate([x1 * cos - x2 * sin, x1 * sin + x2 * cos], axis=-1)
        B, S, D = x.shape
        qkv = x @ w_qkv.T + b_qkv
        Q, K, V = jnp.split(qkv, 3, axis=-1)
        Q, K = (_rope(Q), _rope(K))
        iq = (x @ w_iq.T + b_iq).reshape(B, S, IDX_HEADS, IDX_DIM)
        ik = x @ w_ik.T + b_ik
        iw = x @ w_iw.T + b_iw
        head_scores = jax.nn.relu(jnp.einsum('bqhd,bkd->bhqk', iq, ik))
        index_scores = jnp.einsum('bhqk,bqh->bqk', head_scores, iw)
        k = min(TOP_K, S)
        _, top_idx = jax.lax.top_k(index_scores, k)
        mask = jnp.zeros((B, S, S), dtype=bool)
        mask = mask.at[jnp.arange(B)[:, None, None], jnp.arange(S)[None, :, None], top_idx].set(True)
        attn_bias = jnp.where(mask, 0.0, -jnp.inf)
        scale = 1.0 / np.sqrt(D).astype(np.float32)
        logits = jnp.einsum('bqd,bkd->bqk', Q, K) * scale + attn_bias
        attn = jax.nn.softmax(logits, axis=-1)
        attn_out = jnp.einsum('bqk,bkd->bqd', attn, V)
        return attn_out @ w_o.T + b_o

    def _L0_ffn_ref(x, Wr, W1, b1, W2, b2):
        import jax, jax.numpy as jnp
        import numpy as np
        E = 8
        B, S, H = x.shape
        xf = x.reshape(-1, H)
        probs = jax.nn.softmax(xf @ Wr.T, axis=-1)
        eid = E - 1
        h = jax.nn.gelu(xf @ W1[eid] + b1[eid], approximate=False)
        y = (h @ W2[eid] + b2[eid]) * probs[:, eid:eid + 1]
        return y.reshape(B, S, H)
    x = L0_attn_x
    x = x + 0.5 * _L0_ffn_ref(_layernorm(x, axis=-1), L0_ffn_Wr, L0_ffn_W1, L0_ffn_b1, L0_ffn_W2, L0_ffn_b2)
    x = x + _L0_attn_ref(_layernorm(x, axis=-1), L0_attn_w_qkv, L0_attn_b_qkv, L0_attn_w_o, L0_attn_b_o, L0_attn_w_iq, L0_attn_b_iq, L0_attn_w_ik, L0_attn_b_ik, L0_attn_w_iw, L0_attn_b_iw)
    x = x + 0.5 * _L0_ffn_ref(_layernorm(x, axis=-1), L0_ffn_Wr, L0_ffn_W1, L0_ffn_b1, L0_ffn_W2, L0_ffn_b2)
    return x

_drawn_inputs = setup_inputs


def setup_inputs(seed=0):
    import zlib

    import numpy as np

    out = dict(_drawn_inputs(seed))
    spreads = {'L0_attn_b_qkv': (0.0, 0.289),
     'L0_attn_b_o': (0.0, 0.1),
     'L0_attn_b_iq': (0.0, 0.761),
     'L0_attn_b_ik': (0.0, 0.8),
     'L0_attn_b_iw': (0.0, 0.623),
     'L0_ffn_b1': (0.0, 0.8),
     'L0_ffn_b2': (0.0, 0.616)}
    factors = {'L0_attn_w_qkv': 3.008,
     'L0_attn_w_iq': 3.05,
     'L0_attn_w_ik': 2.983,
     'L0_attn_w_iw': 3.386,
     'L0_ffn_Wr': 8.0,
     'L0_ffn_W1': 4.086,
     'L0_ffn_W2': 3.805}
    for name, (base, spread) in spreads.items():
        noise = np.random.default_rng([zlib.crc32(name.encode()), seed]).standard_normal(out[name].shape)
        drawn = base * np.exp(spread * noise) if base else spread * noise
        out[name] = jnp.asarray(drawn.astype(out[name].dtype))
    for name, factor in factors.items():
        out[name] = (out[name] * factor).astype(out[name].dtype)
    return out
```

```python
import concourse.bass as bass
from concourse import mybir
from contextlib import ExitStack
import numpy as np

FP32 = mybir.dt.float32
FP32R = mybir.dt.float32r
BF16 = mybir.dt.bfloat16
I32 = mybir.dt.int32
ALU = mybir.AluOpType
ACT = mybir.ActivationFunctionType
AX = mybir.AxisListType

P = 128
BATCH, SEQ, D = 4, 2048, 256
ROWS = BATCH * SEQ
DC = D // P
F = 1024
FC = F // P
E = 8
IH, ID = 4, 64
TOPK = 64
EPS = 1e-5

GR = 512
RT = GR // P
NG = ROWS // GR
NT = ROWS // P
TB = SEQ // P
KN = 512
NKN = SEQ // KN
HALF = SEQ // 2
GRP = 128
NGRP = SEQ // GRP
NCAND = NGRP * 8 + 8
NEG = -(2.0 ** 100)
TIE = -(2.0 ** -100)
TAKEN = -3.0e38
SCALE = 1.0 / 16.0


class Tensors:
    pass


def sb(ctx, nc, name, shape, dt=FP32):
    return ctx.enter_context(nc.sbuf_tensor(name, shape, dt))


def psum(ctx, nc, name, shape, dt=FP32):
    return ctx.enter_context(nc.psum_tensor(name, shape, dt))


def sem(ctx, nc, name):
    return ctx.enter_context(nc.semaphore(name))


def f32(ap):
    return ap.bitcast(FP32)


def macaron_kernel(nc, d):
    d.kT = nc.dram_tensor("kT_scratch", [2, DC, P, ROWS], FP32).ap()
    d.qT = nc.dram_tensor("qT_scratch", [NT, P, 2, DC, P], FP32).ap()
    d.v = nc.dram_tensor("v_scratch", [2, P, NT, D], FP32).ap()
    d.ik = nc.dram_tensor("ik_scratch", [2, ID, ROWS], FP32).ap()
    d.iq = nc.dram_tensor("iq_scratch", [NT, 2, ID, IH, P], FP32).ap()
    d.iw = nc.dram_tensor("iw_scratch", [P, NT, IH], FP32).ap()
    d.x1 = nc.dram_tensor("x1_scratch", [ROWS, D], FP32).ap()
    d.x2 = nc.dram_tensor("x2_scratch", [ROWS, D], FP32).ap()

    with ExitStack() as outer:
        w = Tensors()
        w.w1h = sb(outer, nc, "w1h", [P, DC, F], FP32R)
        w.w1l = sb(outer, nc, "w1l", [P, DC, F], FP32R)
        w.w2h = sb(outer, nc, "w2h", [P, FC, D], FP32R)
        w.w2l = sb(outer, nc, "w2l", [P, FC, D], FP32R)
        w.wrh = sb(outer, nc, "wrh", [P, DC, E], FP32R)
        w.wrl = sb(outer, nc, "wrl", [P, DC, E], FP32R)
        w.b1c = sb(outer, nc, "b1c", [P, FC])
        w.b2b = sb(outer, nc, "b2b", [P, D])
        w.bvo = sb(outer, nc, "bvo", [P, D])
        w.ident = sb(outer, nc, "ident", [P, P])
        w.mhalf = sb(outer, nc, "mhalf", [P, RT])
        w.epsilon = sb(outer, nc, "epsilon", [P, RT])
        with ExitStack() as proj:
            w.wqkh = sb(proj, nc, "wqkh", [P, DC, 2 * D], FP32R)
            w.wqkl = sb(proj, nc, "wqkl", [P, DC, 2 * D], FP32R)
            w.wiqh = sb(proj, nc, "wiqh", [P, DC, D], FP32R)
            w.wiql = sb(proj, nc, "wiql", [P, DC, D], FP32R)
            w.wikh = sb(proj, nc, "wikh", [P, DC, ID], FP32R)
            w.wikl = sb(proj, nc, "wikl", [P, DC, ID], FP32R)
            w.wvwh = sb(proj, nc, "wvwh", [P, DC, D + IH], FP32R)
            w.wvwl = sb(proj, nc, "wvwl", [P, DC, D + IH], FP32R)
            w.bqkc = sb(proj, nc, "bqkc", [P, 2 * DC])
            w.biqc = sb(proj, nc, "biqc", [P, DC])
            w.bikc = sb(proj, nc, "bikc", [ID, 1])
            w.biwb = sb(proj, nc, "biwb", [P, IH])
            setup(nc, d, w)
            ffn_phase(nc, d, w, "a", d.x, d.x1)
        attention_phase(nc, d, w)
        ffn_phase(nc, d, w, "c", d.x2, d.out)


def setup(nc, d, w):
    with ExitStack() as ctx:
        w1f = sb(ctx, nc, "w1f", [P, DC, F])
        w2f = sb(ctx, nc, "w2f", [P, FC, D])
        wrf = sb(ctx, nc, "wrf", [P, DC, E])
        wqkf = sb(ctx, nc, "wqkf", [P, DC, 2 * D])
        wiqf = sb(ctx, nc, "wiqf", [P, DC, D])
        wikf = sb(ctx, nc, "wikf", [P, DC, ID])
        wvwf = sb(ctx, nc, "wvwf", [P, DC, D + IH])
        wvf = sb(ctx, nc, "wvf", [P, DC, D])
        wof = sb(ctx, nc, "wof", [P, DC, D])
        bvc = sb(ctx, nc, "bvc", [P, DC])
        bvm = sb(ctx, nc, "bvm", [P, DC, P])
        bob = sb(ctx, nc, "bob", [P, D])
        vo_ps = psum(ctx, nc, "vo_ps", [P, DC, D])
        bvo_ps = psum(ctx, nc, "bvo_ps", [P, D])
        vo_loaded = sem(ctx, nc, "vo_loaded")
        w_loaded = sem(ctx, nc, "w_loaded")
        c_loaded = sem(ctx, nc, "c_loaded")
        ident_set = sem(ctx, nc, "ident_set")
        bvm_set = sem(ctx, nc, "bvm_set")
        vo_done = sem(ctx, nc, "vo_done")
        vo_copied = sem(ctx, nc, "vo_copied")
        block = ctx.enter_context(nc.Block())

        def chunks(ap):
            return ap.rearrange("(c p) n -> p c n", p=P)

        weights = [(wqkf, d.wqkT), (wiqf, d.wiqT), (wikf, d.wikT), (w1f, d.w1), (w2f, d.w2), (wrf, d.wrT)]

        @block.sync
        def _(sp):
            sp.dma_start(wvf[:], chunks(d.wv)).then_inc(vo_loaded, 16)
            sp.dma_start(wof[:], chunks(d.woT)).then_inc(vo_loaded, 16)
            with nc.allow_non_contiguous_dma(reason="small weights and biases, once"):
                sp.dma_start(bvc[:], d.bv.rearrange("(c p) -> p c", p=P)).then_inc(vo_loaded, 16)
                sp.dma_start(wvwf[:, :, D:D + IH], chunks(d.wiwT)).then_inc(w_loaded, 16)
                for to, of in weights:
                    sp.dma_start(to[:], chunks(of)).then_inc(w_loaded, 16)
                for to, of in ((w.b1c, d.b1), (w.bqkc, d.bqk), (w.biqc, d.biq)):
                    sp.dma_start(to[:], of.rearrange("(c p) -> p c", p=P)).then_inc(c_loaded, 16)
                sp.dma_start(w.bikc[:], d.bik.unsqueeze(1)).then_inc(c_loaded, 16)
                sp.dma_start(w.biwb[:], d.biw.partition_broadcast(P)).then_inc(c_loaded, 16)
                sp.dma_start(w.b2b[:], d.b2.partition_broadcast(P)).then_inc(c_loaded, 16)
                sp.dma_start(bob[:], d.bo.partition_broadcast(P)).then_inc(c_loaded, 16)
            sp.wait_ge(c_loaded, 16 * 7)

        @block.gpsimd
        def _(pool):
            pool.memset(w.mhalf[:], -0.5)
            pool.memset(w.epsilon[:], EPS)
            pool.memset(w.ident[:], 0.0).then_inc(ident_set, 1)
            pool.wait_ge(ident_set, 1)
            pool.affine_select(out=w.ident[:], in_=w.ident[:], compare_op=ALU.not_equal, fill=1.0,
                               base=0, pattern=[[-1, P]], channel_multiplier=1)

        @block.tensor
        def _(pe):
            pe.wait_ge(vo_loaded, 48)
            for n in range(DC):
                for c in range(DC):
                    pe.matmul(vo_ps[:, n, :], wvf[:, c, n * P:(n + 1) * P], wof[:, c, :],
                              start=(c == 0), stop=(c == DC - 1)).then_inc(vo_done, 1)
            pe.wait_ge(bvm_set, DC)
            for c in range(DC):
                pe.matmul(bvo_ps[:], bvm[:, c, :], wof[:, c, :],
                          start=(c == 0), stop=(c == DC - 1)).then_inc(vo_done, 1)

        @block.vector
        def _(dve):
            dve.wait_ge(vo_loaded, 48)
            for c in range(DC):
                dve.tensor_copy(bvm[:, c, :], bvc[:, c:c + 1].to_broadcast([P, P])).then_inc(bvm_set, 1)
            dve.wait_ge(vo_done, DC * DC)
            for n in range(DC):
                dve.tensor_copy(wvwf[:, n, 0:D], vo_ps[:, n, :]).then_inc(vo_copied, 1)
            dve.wait_ge(vo_done, DC * DC + DC)
            dve.wait_ge(c_loaded, 16 * 7)
            dve.tensor_tensor(w.bvo[:], bvo_ps[:], bob[:], ALU.add)
            dve.wait_ge(w_loaded, 16 * (1 + len(weights)))
            dve.wait_ge(vo_copied, DC)
            parts = [(wvwf, w.wvwh, w.wvwl), (wqkf, w.wqkh, w.wqkl), (wiqf, w.wiqh, w.wiql),
                     (wikf, w.wikh, w.wikl), (w1f, w.w1h, w.w1l), (w2f, w.w2h, w.w2l), (wrf, w.wrh, w.wrl)]
            for whole, high, _ in parts:
                dve.tensor_copy(high[:], whole[:]).then_inc(vo_copied, 1)
            for n, (whole, high, low) in enumerate(parts):
                dve.wait_ge(vo_copied, DC + n + 1)
                dve.tensor_tensor(low[:], whole[:], f32(high[:]), ALU.subtract)


def ffn_phase(nc, d, w, phase, src, dst):
    with_proj = phase == "a"
    with ExitStack() as ctx:
        def buf(name, shape, dt=FP32):
            return sb(ctx, nc, name + phase, shape, dt)

        def bank(name, shape, dt=FP32):
            return psum(ctx, nc, name + phase, shape, dt)

        def count(name):
            return sem(ctx, nc, name + "_" + phase)

        xa = buf("xa", [P, RT, D])
        xr = buf("xr", [P, RT, D])
        xn = buf("xn", [P, RT, D])
        xTh = buf("xTh", [P, DC, GR], FP32R)
        xTl = buf("xTl", [P, DC, GR], FP32R)
        hf = buf("hf", [P, 2, GR])
        hh = buf("hh", [P, FC, GR], FP32R)
        hl = buf("hl", [P, FC, GR], FP32R)
        rs = buf("rs", [E, GR])
        re = buf("re", [P, RT, E])
        rx = buf("rx", [P, RT, E])
        rm = buf("rm", [P, RT])
        rsum = buf("rsum", [P, RT])
        rinv = buf("rinv", [P, RT])
        pr = buf("pr", [P, RT])
        st = buf("st", [P, RT, 6])
        mv = buf("mv", [P, RT, 2])
        ve = buf("ve", [P, RT])
        rstd = buf("rstd", [P, RT])
        yb = buf("yb", [P, 2, D])
        xo = buf("xo", [P, RT, D])
        if with_proj:
            x1b = buf("x1b", [P, RT, D])
            xn2 = buf("xn2", [P, RT, D])
            yTh = buf("yTh", [P, DC, GR], FP32R)
            yTl = buf("yTl", [P, DC, GR], FP32R)
            st2 = buf("st2", [P, RT, 6])
            mv2 = buf("mv2", [P, RT, 2])
            ve2 = buf("ve2", [P, RT])
            rstd2 = buf("rstd2", [P, RT])
            cs = buf("cs", [P, 2, GR])
            raw = buf("raw", [P, DC, GR])
            rc = buf("rc", [P, DC, GR])
            rsn = buf("rsn", [P, DC, GR])
            rot = buf("rot", [P, DC, GR])
            qh = buf("qh", [P, DC, GR], FP32R)
            ql = buf("ql", [P, DC, GR], FP32R)
            iqf = buf("iqf", [P, DC, GR])
            iqh = buf("iqh", [P, DC, GR], FP32R)
            iql = buf("iql", [P, DC, GR], FP32R)
            ikf = buf("ikf", [ID, GR])
            ikh = buf("ikh", [ID, GR], FP32R)
            ikl = buf("ikl", [ID, GR], FP32R)
            vh = buf("vh", [P, RT, D], FP32R)
            vl = buf("vl", [P, RT, D], FP32R)
            iw = buf("iw", [P, RT, IH])

        tp = bank("tp", [P, DC, GR])
        hp = bank("hp", [P, 2, GR])
        yp = bank("yp", [P, RT, D])
        rp = bank("rp", [P, GR])
        rt = bank("rt", [P, RT, E])
        yT = yp[:].rearrange("p r d -> p (r d)").rearrange("p (c n) -> p c n", c=DC)

        xa_loaded = count("xa_loaded")
        xr_loaded = count("xr_loaded")
        stats = count("stats")
        rstd_set = count("rstd_set")
        xn_set = count("xn_set")
        xT_done = count("xT_done")
        xTh_set = count("xTh_set")
        xTl_set = count("xTl_set")
        router_done = count("router_done")
        rs_set = count("rs_set")
        rt_done = count("rt_done")
        rx_set = count("rx_set")
        re_set = count("re_set")
        h_done = count("h_done")
        hf_set = count("hf_set")
        hh_set = count("hh_set")
        hl_set = count("hl_set")
        y_done = count("y_done")
        xo_set = count("xo_set")
        xo_stored = count("xo_stored")
        dve_step = count("dve_step")
        pool_step = count("pool_step")
        act_step = count("act_step")
        if with_proj:
            cs_loaded = count("cs_loaded")
            stats2 = count("stats2")
            rstd2_set = count("rstd2_set")
            xn2_set = count("xn2_set")
            yT_done = count("yT_done")
            yTh_set = count("yTh_set")
            yTl_set = count("yTl_set")
            x1b_set = count("x1b_set")
            p_done = count("p_done")
            p_read = count("p_read")
            raw_set = count("raw_set")
            rc_set = count("rc_set")
            rot_set = count("rot_set")
            qh_set = count("qh_set")
            ql_set = count("ql_set")
            iq_set = count("iq_set")
            iql_set = count("iql_set")
            ik_set = count("ik_set")
            ikl_set = count("ikl_set")
            vh_set = count("vh_set")
            q_stored = count("q_stored")
            iq_stored = count("iq_stored")
            v_stored = count("v_stored")
        block = ctx.enter_context(nc.Block())

        NP = 2 * DC + DC + 1 + RT

        def row_tiles(dram, row):
            return dram[bass.ds(row, GR), :].rearrange("(r p) d -> p r d", p=P)

        @block.sync
        def _(sp):
            def at(v):
                return v if isinstance(v, int) else sp.snap(v)

            def load_xa(g):
                row = at(g * GR)
                if not isinstance(g, int) or g > 0:
                    sp.wait_ge(xn_set, at(g * RT))
                sp.dma_start(xa[:], row_tiles(src, row)).then_inc(xa_loaded, 16)

            def load_xr(g):
                row = at(g * GR)
                if not isinstance(g, int) or g > 0:
                    sp.wait_ge(xo_set, at(g * RT))
                sp.dma_start(xr[:], row_tiles(src, row)).then_inc(xr_loaded, 16)

            def store_xo(g):
                row = at(g * GR)
                if with_proj:
                    sp.wait_ge(x1b_set, at(g + 1))
                    sp.dma_start(row_tiles(dst, row), x1b[:]).then_inc(xo_stored, 16)
                else:
                    sp.wait_ge(xo_set, at((g + 1) * RT))
                    sp.dma_start(row_tiles(dst, row), xo[:]).then_inc(xo_stored, 16)

            def load_cs(g):
                g = at(g)
                if not isinstance(g, int) or g > 0:
                    sp.wait_ge(rc_set, at(g * 4))
                sp.dma_start(cs[:], d.cs_t[bass.ds(g, 1), :, :, :].rearrange("g p t n -> (g p) t n")
                             ).then_inc(cs_loaded, 16)

            def store_proj(g):
                row, tile = at(g * GR), at(g * RT)
                for which in range(2):
                    sp.wait_ge(ql_set, at(2 * g + which + 1))
                    for part, t in enumerate((qh, ql)):
                        for c in range(DC):
                            if which == 0:
                                to = d.qT[bass.ds(tile, RT), :, part, c, :].rearrange("t p q -> p t q")
                                of = f32(t[:, c, :]).rearrange("p (t q) -> p t q", t=RT)
                            else:
                                to = d.kT[part, c, :, bass.ds(row, GR)]
                                of = f32(t[:, c, :])
                            sp.dma_start(to, of).then_inc(q_stored, 16)
                sp.wait_ge(iql_set, at(g + 1))
                for part, t in enumerate((iqh, iql)):
                    for c in range(DC):
                        for a in range(2):
                            sp.dma_start(
                                d.iq[bass.ds(tile, RT), part, :, 2 * c + a, :].rearrange("t d q -> d t q"),
                                f32(t[a * ID:(a + 1) * ID, c, :]).rearrange("d (t q) -> d t q", t=RT),
                            ).then_inc(iq_stored, 16)
                sp.wait_ge(ikl_set, at(g + 1))
                for part, t in enumerate((ikh, ikl)):
                    sp.dma_start(d.ik[part, :, bass.ds(row, GR)], f32(t[:])).then_inc(iq_stored, 16)
                sp.wait_ge(p_read, at((g + 1) * NP))
                for part, t in enumerate((vh, vl)):
                    sp.dma_start(d.v[part, :, bass.ds(tile, RT), :], f32(t[:])).then_inc(v_stored, 16)
                sp.dma_start(d.iw[:, bass.ds(tile, RT), :], iw[:]).then_inc(v_stored, 16)

            def body(g, first=False, more=2):
                if more > 1:
                    load_xa(g + 2)
                store_xo(g)
                if more > 0:
                    load_xr(g + 1)
                if with_proj:
                    if not first:
                        store_proj(g - 1)
                        load_cs(g)

            load_xa(0)
            load_xr(0)
            if with_proj:
                load_cs(0)
            load_xa(1)
            body(0, first=True)
            with sp.Fori(1, NG - 2) as g:
                body(g)
            body(NG - 2, more=1)
            body(NG - 1, more=0)
            if with_proj:
                store_proj(NG - 1)
                sp.wait_ge(q_stored, NG * 4 * DC * 16)
                sp.wait_ge(iq_stored, NG * (4 * DC + 2) * 16)
                sp.wait_ge(v_stored, NG * 3 * 16)
            sp.wait_ge(xo_stored, NG * 16)

        @block.tensor
        def _(pe):
            def transposes(g, rows, ready, to, done):
                for r in range(RT):
                    pe.wait_ge(ready, g * RT + r + 1)
                    for c in range(DC):
                        ins = pe.transpose(to[:, c, r * P:(r + 1) * P], rows[:, r, c * P:(c + 1) * P], w.ident[:])
                        if r == RT - 1:
                            ins.then_inc(done, 1)

            def three(to, lhs, rhs, start, stop):
                (lh, ll), (rh, rl) = lhs, rhs
                pe.matmul(to, lh, rh, start=start, stop=False)
                pe.matmul(to, ll, rh, start=False, stop=False)
                return pe.matmul(to, lh, rl, start=False, stop=stop)

            def ffn_up(g):
                pe.wait_ge(xTl_set, (g + 1) * DC)
                if not isinstance(g, int) or g > 0:
                    pe.wait_ge(rs_set, g)
                for c in range(DC):
                    ins = three(rp[0:E, :], (w.wrh[:, c, :], w.wrl[:, c, :]), (xTh[:, c, :], xTl[:, c, :]),
                                c == 0, c == DC - 1)
                ins.then_inc(router_done, 1)
                for f in range(FC):
                    if not isinstance(g, int) or g > 0 or f >= 2:
                        pe.wait_ge(hf_set, g * FC + f - 1)
                    if with_proj and f < 2 and (not isinstance(g, int) or g > 1):
                        pe.wait_ge(p_read, (g - 1) * NP)
                    if f == 2:
                        pe.wait_ge(rs_set, g + 1)
                        if not isinstance(g, int) or g > 0:
                            pe.wait_ge(rx_set, g)
                    fs = slice(f * P, (f + 1) * P)
                    for c in range(DC):
                        ins = three(hp[:, f % 2, :], (w.w1h[:, c, fs], w.w1l[:, c, fs]),
                                    (xTh[:, c, :], xTl[:, c, :]), c == 0, c == DC - 1)
                    ins.then_inc(h_done, 1)
                    if f == 2:
                        for r in range(RT):
                            ins = pe.transpose(rt[:, r, :], rs[:, r * P:(r + 1) * P], w.ident[0:E, 0:E])
                        ins.then_inc(rt_done, 1)

            def ffn_down(g):
                if not isinstance(g, int) or g > 0:
                    pe.wait_ge(xo_set, g * RT)
                for r in range(RT):
                    rs_ = slice(r * P, (r + 1) * P)
                    for f in range(FC):
                        if r == 0:
                            pe.wait_ge(hl_set, g * FC + f + 1)
                        ins = three(yp[:, r, :], (hh[:, f, rs_], hl[:, f, rs_]), (w.w2h[:, f, :], w.w2l[:, f, :]),
                                    f == 0, f == FC - 1)
                    ins.then_inc(y_done, 1)

            def project(g):
                pe.wait_ge(yTl_set, (g + 1) * DC)
                n = 0

                def free(n):
                    if n >= 2:
                        pe.wait_ge(p_read, g * NP + n - 1)
                for lo, m, wh, wl in ([(c * P, P, w.wqkh, w.wqkl) for c in range(2 * DC)]
                                      + [(c * P, P, w.wiqh, w.wiql) for c in range(DC)]
                                      + [(0, ID, w.wikh, w.wikl)]):
                    free(n)
                    for c in range(DC):
                        ins = three(hp[0:m, n % 2, :], (wh[:, c, lo:lo + m], wl[:, c, lo:lo + m]),
                                    (yTh[:, c, :], yTl[:, c, :]), c == 0, c == DC - 1)
                    ins.then_inc(p_done, 1)
                    n += 1
                for r in range(RT):
                    free(n)
                    rs_ = slice(r * P, (r + 1) * P)
                    for c in range(DC):
                        ins = three(hp[:, n % 2, 0:D + IH], (yTh[:, c, rs_], yTl[:, c, rs_]),
                                    (w.wvwh[:, c, :], w.wvwl[:, c, :]), c == 0, c == DC - 1)
                    ins.then_inc(p_done, 1)
                    n += 1

            def body(g, first=False, last=False):
                if with_proj and not first:
                    pe.wait_ge(xo_set, g * RT)
                    transposes(g - 1, xn2, xn2_set, yT, yT_done)
                ffn_up(g)
                if not last:
                    transposes(g + 1, xn, xn_set, tp, xT_done)
                if with_proj and not first:
                    pe.wait_ge(yTl_set, g * DC)
                ffn_down(g)
                if with_proj and not first:
                    pe.wait_ge(hf_set, (g + 1) * FC)
                    project(g - 1)

            transposes(0, xn, xn_set, tp, xT_done)
            body(0, first=True)
            body(1)
            with pe.Fori(2, NG - 1) as g:
                body(g)
            body(NG - 1, last=True)
            if with_proj:
                pe.wait_ge(xo_set, NG * RT)
                transposes(NG - 1, xn2, xn2_set, yT, yT_done)
                pe.wait_ge(p_read, (NG - 1) * NP)
                project(NG - 1)

        @block.scalar
        def _(act):
            def split_high(g, bank, done, to, to_set):
                for c in range(DC):
                    act.wait_ge(done, g * DC + c + 1)
                    act.activation(to[:, c, :], bank[:, c, :], ACT.Copy).then_inc(to_set, 1)

            def ffn(g, last=False):
                act.wait_ge(router_done, g + 1)
                act.activation(rs[:], rp[0:E, :], ACT.Copy).then_inc(rs_set, 1)
                for f in range(FC):
                    act.wait_ge(h_done, g * FC + f + 1)
                    if not isinstance(g, int) or g > 0 or f >= 2:
                        act.wait_ge(hl_set, g * FC + f - 1)
                    act.activation(hf[:, f % 2, :], hp[:, f % 2, :], ACT.Gelu,
                                   bias=w.b1c[:, f:f + 1]).then_inc(hf_set, 1)
                if not last:
                    split_high(g + 1, tp, xT_done, xTh, xTh_set)
                act.wait_ge(rx_set, g + 1)
                act.activation(re[:], rx[:], ACT.Exp).then_inc(re_set, 1)

            def project(g):
                for n in range(2 * DC):
                    act.wait_ge(p_done, g * NP + n + 1)
                    if n % DC == 0 and (not isinstance(g, int) or g > 0 or n > 0):
                        act.wait_ge(rc_set, 4 * g + n)
                    act.activation(raw[:, n % DC, :], hp[:, n % 2, :], ACT.Identity,
                                   bias=w.bqkc[:, n:n + 1]).then_inc(p_read, 1)
                for c in range(DC):
                    act.wait_ge(p_done, g * NP + 2 * DC + c + 1)
                    if c == 0 and (not isinstance(g, int) or g > 0):
                        act.wait_ge(iql_set, g)
                        act.wait_ge(iq_stored, g * (4 * DC + 2) * 16)
                    act.activation(iqh[:, c, :], hp[:, c % 2, :], ACT.Identity,
                                   bias=w.biqc[:, c:c + 1]).then_inc(iq_set, 1)
                    act.activation(iqf[:, c, :], hp[:, c % 2, :], ACT.Identity,
                                   bias=w.biqc[:, c:c + 1]).then_inc(p_read, 1)
                act.wait_ge(p_done, g * NP + 3 * DC + 1)
                if not isinstance(g, int) or g > 0:
                    act.wait_ge(ikl_set, g)
                act.activation(ikh[:], hp[0:ID, 0, :], ACT.Identity, bias=w.bikc[:]).then_inc(ik_set, 1)
                act.activation(ikf[:], hp[0:ID, 0, :], ACT.Identity, bias=w.bikc[:]).then_inc(p_read, 1)
                for r in range(RT):
                    act.wait_ge(p_done, g * NP + 3 * DC + r + 2)
                    if r == 0 and (not isinstance(g, int) or g > 0):
                        act.wait_ge(v_stored, g * 3 * 16)
                    act.activation(vh[:, r, :], hp[:, (r + 1) % 2, 0:D], ACT.Copy).then_inc(vh_set, 1)

            def body(g, first=False, last=False):
                if with_proj and not first:
                    split_high(g - 1, yT, yT_done, yTh, yTh_set)
                ffn(g, last)
                if with_proj and not first:
                    project(g - 1)

            split_high(0, tp, xT_done, xTh, xTh_set)
            body(0, first=True)
            with act.Fori(1, NG - 1) as g:
                body(g)
            body(NG - 1, last=True)
            if with_proj:
                split_high(NG - 1, yT, yT_done, yTh, yTh_set)
                project(NG - 1)

        @block.gpsimd
        def _(pool):
            def inverse_std(g, stats, mv, ve, rstd, rstd_set):
                pool.wait_ge(stats, (g + 1) * RT)
                pool.tensor_tensor(ve[:], mv[:, :, 1], w.epsilon[:], ALU.add).then_inc(pool_step, 1)
                pool.wait_ge(pool_step, 1)
                pool.tensor_tensor(rstd[:], ve[:], w.mhalf[:], ALU.pow).then_inc(rstd_set, 1)
                pool.sem_clear(pool_step)

            def rotate(g, which):
                pool.wait_ge(p_read, g * NP + DC * (which + 1))
                if which == 0:
                    pool.wait_ge(cs_loaded, (g + 1) * 16)
                if not isinstance(g, int) or g > 0 or which > 0:
                    pool.wait_ge(rot_set, 4 * g + 2 * which)
                for t, n in ((rc, 0), (rsn, 1)):
                    pool.tensor_tensor(t[:], raw[:], cs[:, n:n + 1, :].to_broadcast([P, DC, GR]),
                                       ALU.mult).then_inc(rc_set, 1)

            def body(g, first=False, last=False):
                if not last:
                    inverse_std(g + 1, stats, mv, ve, rstd, rstd_set)
                if with_proj:
                    inverse_std(g, stats2, mv2, ve2, rstd2, rstd2_set)
                    if not first:
                        pool.wait_ge(xo_stored, g * 16)
                    pool.wait_ge(xo_set, (g + 1) * RT)
                    pool.tensor_tensor(x1b[:], xo[:], w.bvo[:].unsqueeze(1).to_broadcast([P, RT, D]),
                                       ALU.add).then_inc(x1b_set, 1)
                if with_proj and not first:
                    rotate(g - 1, 0)
                    rotate(g - 1, 1)

            inverse_std(0, stats, mv, ve, rstd, rstd_set)
            body(0, first=True)
            with pool.Fori(1, NG - 1) as g:
                body(g)
            body(NG - 1, last=True)
            if with_proj:
                rotate(NG - 1, 0)
                rotate(NG - 1, 1)

        @block.vector
        def _(dve):
            steps = [0]

            def step(ins):
                steps[0] += 1
                ins.then_inc(dve_step, 1)
                return steps[0]

            def clear_steps():
                dve.wait_ge(dve_step, steps[0])
                dve.sem_clear(dve_step)
                steps[0] = 0

            def row_stats(g, rows, st, mv, stats_sem):
                last = [step(dve.bn_stats(st[:, r, :], rows[:, r, :])) for r in range(RT)]
                for r in range(RT):
                    dve.wait_ge(dve_step, last[r])
                    dve.bn_aggr(mv[:, r, :], st[:, r, :]).then_inc(stats_sem, 1)

            def normalise(g, rows, mv, rstd, rstd_set, stats_sem, to, to_set):
                dve.wait_ge(rstd_set, g + 1)
                dve.wait_ge(stats_sem, (g + 1) * RT)
                for r in range(RT):
                    dve.tensor_scalar(to[:, r, :], rows[:, r, :], mv[:, r, 0:1], rstd[:, r:r + 1],
                                      ALU.subtract, ALU.mult).then_inc(to_set, 1)

            def split_low(g, bank, high, high_set, low, low_set):
                for c in range(DC):
                    dve.wait_ge(high_set, g * DC + c + 1)
                    dve.tensor_tensor(low[:, c, :], bank[:, c, :], f32(high[:, c, :]),
                                      ALU.subtract).then_inc(low_set, 1)

            def split_hidden(g, f):
                dve.wait_ge(hf_set, g * FC + f + 1)
                if f == 0 and (not isinstance(g, int) or g > 0):
                    dve.wait_ge(y_done, g * RT)
                dve.tensor_copy(hh[:, f, :], hf[:, f % 2, :]).then_inc(hh_set, 1)
                dve.wait_ge(hh_set, g * FC + f + 1)
                dve.tensor_tensor(hl[:, f, :], hf[:, f % 2, :], f32(hh[:, f, :]), ALU.subtract).then_inc(hl_set, 1)

            def router_max(g):
                dve.wait_ge(rt_done, g + 1)
                n = step(dve.reduce_max(rm[:], rt[:], AX.X))
                dve.wait_ge(dve_step, n)
                dve.tensor_tensor(rx[:], rt[:], rm[:].unsqueeze(2).to_broadcast([P, RT, E]),
                                  ALU.subtract).then_inc(rx_set, 1)

            def router_prob(g):
                dve.wait_ge(re_set, g + 1)
                n = step(dve.reduce_sum(rsum[:], re[:], AX.X))
                dve.wait_ge(dve_step, n)
                n = step(dve.reciprocal(rinv[:], rsum[:]))
                dve.wait_ge(dve_step, n)
                return step(dve.scalar_tensor_tensor(pr[:], re[:, :, E - 1], 0.5, rinv[:], ALU.mult, ALU.mult))

            def residual(g, prob_step):
                dve.wait_ge(xr_loaded, (g + 1) * 16)
                if not with_proj and (not isinstance(g, int) or g > 0):
                    dve.wait_ge(xo_stored, g * 16)
                if with_proj and (not isinstance(g, int) or g > 0):
                    dve.wait_ge(x1b_set, g)
                dve.wait_ge(dve_step, prob_step)
                for r in range(RT):
                    dve.wait_ge(y_done, g * RT + r // 2 * 2 + 2)
                    n = step(dve.tensor_tensor(yb[:, r % 2, :], yp[:, r, :], w.b2b[:], ALU.add))
                    dve.wait_ge(dve_step, n)
                    dve.scalar_tensor_tensor(xo[:, r, :], yb[:, r % 2, :], pr[:, r:r + 1], xr[:, r, :],
                                             ALU.mult, ALU.add).then_inc(xo_set, 1)

            def rotated(g, which):
                dve.wait_ge(rc_set, 4 * g + 2 * which + 2)
                if not isinstance(g, int) or g > 0 or which > 0:
                    dve.wait_ge(q_stored, (2 * g + which) * 2 * DC * 16)
                dve.tensor_tensor(rot[:, 0, :], rc[:, 0, :], rsn[:, 1, :], ALU.subtract).then_inc(rot_set, 1)
                dve.tensor_tensor(rot[:, 1, :], rsn[:, 0, :], rc[:, 1, :], ALU.add).then_inc(rot_set, 1)
                dve.wait_ge(rot_set, 4 * g + 2 * which + 2)
                dve.tensor_copy(qh[:], rot[:]).then_inc(qh_set, 1)
                dve.wait_ge(qh_set, 2 * g + which + 1)
                dve.tensor_tensor(ql[:], rot[:], f32(qh[:]), ALU.subtract).then_inc(ql_set, 1)

            def project(g):
                rotated(g, 1)
                dve.wait_ge(iq_set, (g + 1) * DC)
                dve.wait_ge(p_read, g * NP + 3 * DC)
                if not isinstance(g, int) or g > 0:
                    dve.wait_ge(iq_stored, g * (4 * DC + 2) * 16)
                dve.tensor_tensor(iql[:], iqf[:], f32(iqh[:]), ALU.subtract).then_inc(iql_set, 1)
                dve.wait_ge(ik_set, g + 1)
                dve.wait_ge(p_read, g * NP + 3 * DC + 1)
                dve.tensor_tensor(ikl[:], ikf[:], f32(ikh[:]), ALU.subtract).then_inc(ikl_set, 1)
                if not isinstance(g, int) or g > 0:
                    dve.wait_ge(v_stored, g * 3 * 16)
                for r in range(RT):
                    bank = hp[:, (r + 1) % 2, :]
                    dve.wait_ge(vh_set, g * RT + r + 1)
                    dve.tensor_tensor(iw[:, r, :], bank[:, D:D + IH], w.biwb[:], ALU.add)
                    dve.tensor_tensor(vl[:, r, :], bank[:, 0:D], f32(vh[:, r, :]), ALU.subtract).then_inc(p_read, 1)

            def body(g, first=False, last=False):
                if with_proj and not first:
                    split_low(g - 1, yT, yTh, yTh_set, yTl, yTl_set)
                for f in range(FC):
                    split_hidden(g, f)
                    if f == 1 and not last:
                        dve.wait_ge(xa_loaded, (g + 2) * 16)
                        row_stats(g + 1, xa, st, mv, stats)
                    if f == 4:
                        router_max(g)
                    if f == 5 and not last:
                        normalise(g + 1, xa, mv, rstd, rstd_set, stats, xn, xn_set)
                if not last:
                    split_low(g + 1, tp, xTh, xTh_set, xTl, xTl_set)
                n = router_prob(g)
                residual(g, n)
                if with_proj:
                    dve.wait_ge(xo_set, (g + 1) * RT)
                    row_stats(g, xo, st2, mv2, stats2)
                    if not first:
                        rotated(g - 1, 0)
                    normalise(g, xo, mv2, rstd2, rstd2_set, stats2, xn2, xn2_set)
                    if not first:
                        project(g - 1)
                clear_steps()

            dve.wait_ge(xa_loaded, 16)
            row_stats(0, xa, st, mv, stats)
            normalise(0, xa, mv, rstd, rstd_set, stats, xn, xn_set)
            split_low(0, tp, xTh, xTh_set, xTl, xTl_set)
            clear_steps()
            body(0, first=True)
            with dve.Fori(1, NG - 1) as g:
                body(g)
            body(NG - 1, last=True)
            if with_proj:
                split_low(NG - 1, yT, yTh, yTh_set, yTl, yTl_set)
                rotated(NG - 1, 0)
                project(NG - 1)


def attention_phase(nc, d, w):
    UNITS = [(3, 0), (2, 0), (3, 1), (2, 1), (1, 0), (0, 0), (1, 1), (0, 1)]
    NU = len(UNITS)
    ALL_OUT = NEG * P * (SEQ - TOPK)
    with ExitStack() as ctx:
        def buf(name, shape, dt=FP32):
            return sb(ctx, nc, name, shape, dt)

        def bank(name, shape, dt=FP32):
            return psum(ctx, nc, name, shape, dt)

        def count(name):
            return sem(ctx, nc, "att_" + name)

        kT = buf("kT", [P, 2, DC, SEQ], FP32R)
        v = buf("v", [P, 2, TB, D], FP32R)
        ik = buf("ik", [P, SEQ], FP32R)
        iq = buf("iq", [P, 2, IH, P], FP32R)
        qT = buf("qT", [P, 2, DC, P], FP32R)
        iwp = buf("iwp", [P, IH])
        iwd = buf("iwd", [P, IH])
        x1t = buf("x1t", [P, D])
        x2t = buf("x2t", [P, D])
        r01 = buf("r01", [P, 2, SEQ])
        r23 = buf("r23", [P, 2, SEQ])
        u = buf("u", [P, SEQ])
        tie = buf("tie", [P, HALF])
        tie_i = buf("tie_i", [P, HALF], I32)
        sc = buf("sc", [P, SEQ])
        rest = buf("rest", [P, SEQ])
        cand = buf("cand", [P, NCAND])
        best = buf("best", [P, 8])
        bias = buf("bias", [P, SEQ], BF16)
        cnt = buf("cnt", [P, 1])
        ones = buf("ones", [P, 1])
        gate = buf("gate", [P, 2])
        dve_gate = buf("dve_gate", [1, NKN])
        redo = buf("redo", [1, 1], I32)
        pr = buf("pr", [P, SEQ])
        mx = buf("mx", [P, NKN])
        nm = buf("nm", [P, 1])
        rsum = buf("rsum_t", [P, 1])
        rinv = buf("rinv_t", [P, 1])
        pTh = buf("pTh", [P, 2, KN], FP32R)
        pTl = buf("pTl", [P, 2, KN], FP32R)

        zp = bank("zp", [P, 2, HALF])
        lp = bank("lp", [P, 2, KN])
        pt = bank("pt", [P, KN])
        op = bank("op", [P, KN])

        ik_loaded = count("ik_loaded")
        k_loaded = count("k_loaded")
        v_loaded = count("v_loaded")
        iq_loaded = count("iq_loaded")
        iwp_loaded = count("iwp_loaded")
        iwd_loaded = count("iwd_loaded")
        q_loaded = count("q_loaded")
        x1_loaded = count("x1_loaded")
        x2_stored = count("x2_stored")
        z_done = count("z_done")
        relu_set = count("relu_set")
        u_set = count("u_set")
        s_set = count("s_set")
        bias_set = count("bias_set")
        cnt_set = count("cnt_set")
        check_done = count("check_done")
        l_done = count("l_done")
        m_set = count("m_set")
        nm_set = count("nm_set")
        p_set = count("p_set")
        pt_done = count("pt_done")
        pth_set = count("pth_set")
        ptl_set = count("ptl_set")
        o_done = count("o_done")
        x2_set = count("x2_set")
        dve_step = count("dve_step")
        redo_step = count("redo_step")
        pool_step = count("pool_step")
        const_set = count("const_set")
        block = ctx.enter_context(nc.Block())

        @block.sync
        def _(sp):
            def at(v):
                return v if isinstance(v, int) else sp.snap(v)

            def positive(g):
                return not isinstance(g, int) or g > 0

            def load_ik(b):
                row = at(b * SEQ)
                if positive(b):
                    sp.wait_ge(z_done, at(b * TB * NU))
                for part in range(2):
                    sp.dma_start(f32(ik[part * ID:(part + 1) * ID, :]),
                                 d.ik[part, :, bass.ds(row, SEQ)]).then_inc(ik_loaded, 16)

            def load_k(b):
                row = at(b * SEQ)
                if positive(b):
                    sp.wait_ge(l_done, at(b * TB * NKN))
                for part in range(2):
                    for c in range(DC):
                        sp.dma_start(f32(kT[:, part, c, :]),
                                     d.kT[part, c, :, bass.ds(row, SEQ)]).then_inc(k_loaded, 16)

            def load_v(b):
                row = at(b * TB)
                if positive(b):
                    sp.wait_ge(o_done, at(b * TB * NKN))
                for part in range(2):
                    sp.dma_start(f32(v[:, part, :, :]),
                                 d.v[part, :, bass.ds(row, TB), :]).then_inc(v_loaded, 16)

            def load_iq(i):
                i = at(i)
                if positive(i):
                    sp.wait_ge(z_done, at(i * NU))
                for a in range(2):
                    sp.dma_start(f32(iq[a * ID:(a + 1) * ID, :, :, :]),
                                 d.iq[bass.ds(i, 1), :, :, :, :].rearrange("t part d h q -> (t d) part h q")
                                 ).then_inc(iq_loaded, 16)

            def load_iwp(i):
                i = at(i)
                if positive(i):
                    sp.wait_ge(u_set, at(i * 2))
                sp.dma_start(iwp[:], d.iw[:, bass.ds(i, 1), :].rearrange("p t h -> p (t h)")).then_inc(iwp_loaded, 16)

            def load_iwd(i):
                i = at(i)
                if positive(i):
                    sp.wait_ge(s_set, at(i * 2))
                sp.dma_start(iwd[:], d.iw[:, bass.ds(i, 1), :].rearrange("p t h -> p (t h)")).then_inc(iwd_loaded, 16)

            def load_q(i):
                i = at(i)
                if positive(i):
                    sp.wait_ge(l_done, at(i * NKN))
                sp.dma_start(f32(qT[:]), d.qT[bass.ds(i, 1), :, :, :, :].rearrange("t p a c q -> (t p) a c q")
                             ).then_inc(q_loaded, 16)

            def load_x1(i):
                row = at(i * P)
                if positive(i):
                    sp.wait_ge(x2_set, at(i))
                sp.dma_start(x1t[:], d.x1[bass.ds(row, P), :]).then_inc(x1_loaded, 16)

            def store_x2(i):
                row = at(i * P)
                sp.wait_ge(x2_set, at(i + 1))
                sp.dma_start(d.x2[bass.ds(row, P), :], x2t[:]).then_inc(x2_stored, 16)

            def tile(i, b, j, first=False, more=3):
                if j == 1:
                    load_v(b)
                if j == 0:
                    load_k(b)
                load_q(i)
                if not first:
                    load_x1(i - 1)
                if more > 0:
                    load_iwd(i + 1)
                if more > 1:
                    if j == TB - 2:
                        load_ik(b + 1)
                    load_iq(i + 2)
                    load_iwp(i + 2)
                if not first:
                    store_x2(i - 1)

            def batch(b, first=False, last=False):
                tile(b * TB, b, 0, first=first)
                tile(b * TB + 1, b, 1)
                with sp.Fori(2, TB - 2) as j:
                    tile(b * TB + j, b, None)
                tile(b * TB + TB - 2, b, TB - 2, more=1 if last else 3)
                tile(b * TB + TB - 1, b, None, more=0 if last else 3)

            load_ik(0)
            load_iq(0)
            load_iwp(0)
            load_iwd(0)
            load_iq(1)
            load_iwp(1)
            batch(0, first=True)
            with sp.Fori(1, BATCH - 1) as b:
                batch(b)
            batch(BATCH - 1, last=True)
            load_x1(NT - 1)
            store_x2(NT - 1)
            sp.wait_ge(x2_stored, NT * 16)

        @block.tensor
        def _(pe):
            def three(to, lhs, rhs, start, stop):
                (lh, ll), (rh, rl) = lhs, rhs
                pe.matmul(to, lh, rh, start=start, stop=False)
                pe.matmul(to, ll, rh, start=False, stop=False)
                return pe.matmul(to, lh, rl, start=False, stop=stop)

            def score_unit(i, n):
                head, half = UNITS[n]
                if n == 0:
                    pe.wait_ge(iq_loaded, (i + 1) * 32)
                    pe.wait_ge(ik_loaded, (i // TB + 1) * 32)
                if not isinstance(i, int) or i > 0 or n > 1:
                    pe.wait_ge(relu_set, i * NU + n - 1)
                for k in range(2):
                    keys = slice(half * HALF + k * KN, half * HALF + (k + 1) * KN)
                    for part in range(2):
                        ins = pe.matmul(zp[:, n % 2, k * KN:(k + 1) * KN], iq[:, part, head, :], ik[:, keys],
                                        start=(part == 0), stop=(part == 1))
                ins.then_inc(z_done, 1)

            def transposes(i, c):
                if c == 0:
                    pe.wait_ge(p_set, i + 1)
                if not isinstance(i, int) or i > 0 or c > 0:
                    pe.wait_ge(ptl_set, i * NKN + c)
                for k in range(4):
                    keys = slice(c * KN + k * P, c * KN + (k + 1) * P)
                    ins = pe.transpose(pt[:, k * P:(k + 1) * P], pr[:, keys], w.ident[:])
                ins.then_inc(pt_done, 1)

            def values(i, c):
                if c == 0:
                    pe.wait_ge(v_loaded, (i // TB + 1) * 32)
                    if not isinstance(i, int) or i > 0:
                        pe.wait_ge(x2_set, i)
                pe.wait_ge(ptl_set, i * NKN + c + 1)
                for k in range(4):
                    kc = c * 4 + k
                    ks = slice(k * P, (k + 1) * P)
                    ins = three(op[:, 0:D], (pTh[:, c % 2, ks], pTl[:, c % 2, ks]), (v[:, 0, kc, :], v[:, 1, kc, :]),
                                kc == 0, kc == TB - 1)
                ins.then_inc(o_done, 1)

            def logits(i, banks):
                pe.wait_ge(q_loaded, (i + 1) * 16)
                pe.wait_ge(k_loaded, (i // TB + 1) * 64)
                for n in banks:
                    if not isinstance(i, int) or i > 0 or n > 1:
                        pe.wait_ge(m_set, i * NKN + n - 1)
                    keys = slice(n * KN, (n + 1) * KN)
                    for c in range(DC):
                        ins = three(lp[:, n % 2, :], (qT[:, 0, c, :], qT[:, 1, c, :]),
                                    (kT[:, 0, c, keys], kT[:, 1, c, keys]), c == 0, c == DC - 1)
                    ins.then_inc(l_done, 1)

            def check(i):
                pe.wait_ge(cnt_set, i + 1)
                if not isinstance(i, int) or i > 0:
                    pe.wait_ge(x2_set, i)
                pe.matmul(op[0:1, KN - 1:KN], cnt[:], ones[:], start=True, stop=True).then_inc(check_done, 1)

            def tile(i, first=False, last=False):
                for c in range(NKN):
                    if not first:
                        transposes(i - 1, c)
                    if not last:
                        score_unit(i + 1, 2 * c)
                    if not first and c > 0:
                        values(i - 1, c - 1)
                    if not last:
                        score_unit(i + 1, 2 * c + 1)
                if not first:
                    values(i - 1, NKN - 1)
                logits(i, (0, 1))
                check(i)
                logits(i, (2, 3))

            pe.wait_ge(const_set, 5)
            for n in range(NU):
                score_unit(0, n)
            tile(0, first=True)
            tile(1)
            with pe.Fori(2, NT - 1) as i:
                tile(i)
            tile(NT - 1, last=True)
            for c in range(NKN):
                transposes(NT - 1, c)
                values(NT - 1, c)

        @block.scalar
        def _(act):
            def relu(i, n):
                head, half = UNITS[n]
                keys = slice(half * HALF, (half + 1) * HALF)
                act.wait_ge(z_done, i * NU + n + 1)
                if not isinstance(i, int) or i > 0:
                    if head >= 2:
                        act.wait_ge(u_set, (i - 1) * 2 + half + 1)
                    else:
                        act.wait_ge(s_set, (i - 1) * 2 + half + 1)
                to = (r23 if head >= 2 else r01)[:, head % 2, keys]
                act.activation(to, zp[:, n % 2, :], ACT.Relu).then_inc(relu_set, 1)

            def high(i, c):
                act.wait_ge(pt_done, i * NKN + c + 1)
                if not isinstance(i, int) or i > 0 or c >= 2:
                    act.wait_ge(o_done, i * NKN + c - 1)
                act.activation(pTh[:, c % 2, :], pt[:], ACT.Copy).then_inc(pth_set, 1)

            def exponentials(i):
                act.wait_ge(nm_set, i + 1)
                act.activation(pr[:], pr[:], ACT.Exp, bias=nm[:], accum_out=rsum[:]).then_inc(p_set, 1)

            def left_out(i):
                act.wait_ge(bias_set, i + 1)
                act.activation(bias[:], bias[:], ACT.Copy, accum_out=cnt[:]).then_inc(cnt_set, 1)

            def tile(i, first=False, last=False):
                for c in range(NKN):
                    if not first:
                        high(i - 1, c)
                    if not last:
                        relu(i + 1, 2 * c)
                        relu(i + 1, 2 * c + 1)
                left_out(i)
                exponentials(i)

            for n in range(NU):
                relu(0, n)
            tile(0, first=True)
            tile(1)
            with act.Fori(2, NT - 1) as i:
                tile(i)
            tile(NT - 1, last=True)
            for c in range(NKN):
                high(NT - 1, c)

        @block.gpsimd
        def _(pool):
            pool.memset(ones[:], 1.0).then_inc(const_set, 1)
            pool.iota(tie_i[:], [[1, HALF]], base=0, channel_multiplier=0).then_inc(const_set, 1)
            pool.wait_ge(const_set, 2)
            pool.tensor_scalar(tie[:], tie_i[:], TIE, 0.0, ALU.mult, ALU.add).then_inc(const_set, 3)

            def weigh(i):
                pool.wait_ge(iwp_loaded, (i + 1) * 16)
                n = 0
                for half in range(2):
                    keys = slice(half * HALF, (half + 1) * HALF)
                    pool.wait_ge(relu_set, i * NU + 2 * half + 2)
                    if not isinstance(i, int) or i > 0:
                        pool.wait_ge(s_set, (i - 1) * 2 + half + 1)
                    pool.tensor_tensor(gate[:, half:half + 1], ones[:], ones[:], ALU.mult)
                    pool.tensor_scalar(u[:, keys], r23[:, 1, keys], iwp[:, 3:4], TIE * HALF * half,
                                       ALU.mult, ALU.add).then_inc(pool_step, 1)
                    pool.tensor_scalar(r23[:, 0, keys], r23[:, 0, keys], iwp[:, 2:3], 0.0,
                                       ALU.mult, ALU.add).then_inc(pool_step, 1)
                    pool.wait_ge(pool_step, n + 1)
                    pool.tensor_tensor(u[:, keys], u[:, keys], tie[:], ALU.add).then_inc(pool_step, 1)
                    pool.wait_ge(pool_step, n + 3)
                    pool.tensor_tensor(u[:, keys], u[:, keys], r23[:, 0, keys], ALU.add).then_inc(u_set, 1)
                    n += 3
                pool.sem_clear(pool_step)

            pool.wait_ge(const_set, 5)
            weigh(0)
            with pool.Fori(1, NT) as i:
                weigh(i)

        @block.vector
        def _(dve):
            steps = [0]

            def step(ins):
                steps[0] += 1
                ins.then_inc(dve_step, 1)
                return steps[0]

            def low(i, c):
                dve.wait_ge(pth_set, i * NKN + c + 1)
                if not isinstance(i, int) or i > 0 or c >= 2:
                    dve.wait_ge(o_done, i * NKN + c - 1)
                dve.tensor_tensor(pTl[:, c % 2, :], pt[:], f32(pTh[:, c % 2, :]), ALU.subtract).then_inc(ptl_set, 1)

            def scores(i, half):
                keys = slice(half * HALF, (half + 1) * HALF)
                if half == 0:
                    dve.wait_ge(iwd_loaded, (i + 1) * 16)
                dve.wait_ge(u_set, i * 2 + half + 1)
                dve.wait_ge(relu_set, i * NU + 4 + 2 * half + 2)
                n = step(dve.scalar_tensor_tensor(sc[:, keys], r01[:, 1, keys], iwd[:, 1:2], u[:, keys],
                                                  ALU.mult, ALU.add))
                dve.wait_ge(dve_step, n)
                step(dve.scalar_tensor_tensor(sc[:, keys], r01[:, 0, keys], iwd[:, 0:1], sc[:, keys],
                                              ALU.mult, ALU.add))

            def group_best(i, groups):
                for g in groups:
                    ins = dve.max(cand[:, g * 8:g * 8 + 8], sc[:, g * GRP:(g + 1) * GRP])
                    if g == 0:
                        ins.then_inc(s_set, 2)
                    else:
                        step(ins)

            def group_rest(i, groups, n):
                for g in groups:
                    dve.wait_ge(dve_step, n + max(g, 1))
                    step(dve.match_replace(rest[:, g * GRP:(g + 1) * GRP], cand[:, g * 8:g * 8 + 8],
                                           sc[:, g * GRP:(g + 1) * GRP], TAKEN))

            def threshold(i):
                for r in range(TOPK // 8):
                    n = step(dve.max(best[:], cand[:]))
                    dve.wait_ge(dve_step, n)
                    if r < TOPK // 8 - 1:
                        n = step(dve.match_replace(cand[:], best[:], cand[:], TAKEN))
                        dve.wait_ge(dve_step, n)

            def select_again(i):
                n = 0
                for r in range(TOPK // 8):
                    dve.max(best[:], sc[:]).then_inc(redo_step, 1)
                    dve.wait_ge(redo_step, n + 1)
                    dve.match_replace(sc[:], best[:], sc[:], TAKEN).then_inc(redo_step, 1)
                    dve.wait_ge(redo_step, n + 2)
                    n += 2
                dve.tensor_scalar(bias[:], sc[:], TAKEN, NEG, ALU.not_equal, ALU.mult).then_inc(redo_step, 1)
                dve.wait_ge(redo_step, n + 1)
                dve.sem_clear(redo_step)

            def tile(i, first=False):
                scores(i, 0)
                if not first:
                    low(i - 1, 0)
                scores(i, 1)
                if not first:
                    low(i - 1, 1)
                n = steps[0]
                dve.wait_ge(dve_step, n)
                group_best(i, range(NGRP))
                if not first:
                    low(i - 1, 2)
                group_rest(i, range(NGRP), n)
                if not first:
                    low(i - 1, 3)
                dve.wait_ge(dve_step, steps[0])
                n = step(dve.max(cand[:, NGRP * 8:NCAND], rest[:]))
                dve.wait_ge(dve_step, n)
                threshold(i)
                if not first:
                    output(i - 1)
                dve.tensor_scalar(bias[:], sc[:], best[:, 7:8], NEG, ALU.is_lt, ALU.mult).then_inc(bias_set, 1)
                dve.wait_ge(check_done, i + 1)
                n = step(dve.tensor_scalar(redo[:], op[0:1, KN - 1:KN], ALL_OUT, None, ALU.is_gt))
                dve.wait_ge(dve_step, n)
                again = dve.value_load(redo[0:1, 0:1], min_val=0, max_val=1)
                with dve.If(again != 0):
                    select_again(i)
                mask(i)
                dve.wait_ge(dve_step, steps[0])
                dve.sem_clear(dve_step)
                steps[0] = 0

            def mask(i):
                if not isinstance(i, int) or i > 0:
                    dve.wait_ge(pt_done, i * NKN)
                for n in range(NKN):
                    keys = slice(n * KN, (n + 1) * KN)
                    dve.wait_ge(l_done, i * NKN + n + 1)
                    dve.memset(dve_gate[:, n:n + 1], 0.0)
                    dve.tensor_tensor_reduce(out=pr[:, keys], in0=bias[:, keys], in1=lp[:, n % 2, :], scale=SCALE,
                                             scalar=TAKEN, op0=ALU.add, op1=ALU.max,
                                             accum_out=mx[:, n:n + 1]).then_inc(m_set, 1)
                dve.wait_ge(m_set, (i + 1) * NKN)
                dve.tensor_reduce(nm[:], mx[:], AX.X, ALU.max, negate=True).then_inc(nm_set, 1)

            def output(i):
                dve.wait_ge(p_set, i + 1)
                n = step(dve.reciprocal(rinv[:], rsum[:]))
                dve.wait_ge(x1_loaded, (i + 1) * 16)
                dve.wait_ge(o_done, (i + 1) * NKN)
                if not isinstance(i, int) or i > 0:
                    dve.wait_ge(x2_stored, i * 16)
                dve.wait_ge(dve_step, n)
                dve.scalar_tensor_tensor(x2t[:], op[:, 0:D], rinv[:], x1t[:], ALU.mult, ALU.add).then_inc(x2_set, 1)

            tile(0, first=True)
            tile(1)
            with dve.Fori(2, NT) as i:
                tile(i)
            for c in range(NKN):
                low(NT - 1, c)
            output(NT - 1)


_OUTS = [((BATCH, SEQ, D), "float32")]


def kernel(**inputs):
    import concourse.bacc as _bacc
    from concourse.bass_utils import run_bass_kernel_spmd as _run

    a = {k: np.asarray(v) for k, v in inputs.items()}
    last = E - 1
    w_qkv, b_qkv = a["L0_attn_w_qkv"], a["L0_attn_b_qkv"]
    half = D // 2
    inv_freq = (np.float32(1.0) / np.float32(10000.0) ** (np.arange(half, dtype=np.float32) / np.float32(half)))
    ang = np.arange(SEQ, dtype=np.float32)[None, :] * inv_freq.astype(np.float32)[:, None]
    rotations = np.stack([np.cos(ang), np.sin(ang)], 1).reshape(half, 2, SEQ // GR, GR).transpose(2, 0, 1, 3)
    nc = _bacc.Bacc("TRN2", target_bir_lowering=False, num_devices=1)
    arrays = {}

    def give(name, array):
        array = np.ascontiguousarray(array)
        arrays["in_" + name] = array
        return nc.dram_tensor("in_" + name, array.shape, mybir.dt.from_np(array.dtype), kind="ExternalInput").ap()

    d = Tensors()
    d.x = give("x", a["L0_attn_x"].reshape(ROWS, D))
    d.wqkT = give("wqkT", w_qkv[:2 * D].T)
    d.bqk = give("bqk", b_qkv[:2 * D])
    d.wv = give("wv", w_qkv[2 * D:])
    d.bv = give("bv", b_qkv[2 * D:])
    d.woT = give("woT", a["L0_attn_w_o"].T)
    d.bo = give("bo", a["L0_attn_b_o"])
    d.wiqT = give("wiqT", a["L0_attn_w_iq"].T)
    d.biq = give("biq", a["L0_attn_b_iq"])
    d.wikT = give("wikT", a["L0_attn_w_ik"].T)
    d.bik = give("bik", a["L0_attn_b_ik"])
    d.wiwT = give("wiwT", a["L0_attn_w_iw"].T)
    d.biw = give("biw", a["L0_attn_b_iw"])
    d.wrT = give("wrT", a["L0_ffn_Wr"].T)
    d.w1 = give("w1", a["L0_ffn_W1"][last])
    d.b1 = give("b1", a["L0_ffn_b1"][last])
    d.w2 = give("w2", a["L0_ffn_W2"][last])
    d.b2 = give("b2", a["L0_ffn_b2"][last])
    d.cs_t = give("cs_t", np.tile(rotations, (BATCH, 1, 1, 1)))
    d.out = nc.dram_tensor("out_dram", (ROWS, D), FP32, kind="ExternalOutput").ap()
    macaron_kernel(nc, d)
    r = _run(nc, [arrays], core_ids=[0])
    return r.results[0]["out_dram"].reshape(BATCH, SEQ, D)
```

```python
import concourse.bass as bass
from concourse import mybir
from contextlib import ExitStack
import numpy as np

FP32 = mybir.dt.float32
FP32R = mybir.dt.float32r
BF16 = mybir.dt.bfloat16
I32 = mybir.dt.int32
ALU = mybir.AluOpType
ACT = mybir.ActivationFunctionType
AX = mybir.AxisListType

P = 128
BATCH, SEQ, D = 4, 2048, 256
ROWS = BATCH * SEQ
DC = D // P
F = 1024
FC = F // P
E = 8
IH, ID = 4, 64
TOPK = 64
EPS = 1e-5

GR = 512
RT = GR // P
NG = ROWS // GR
NT = ROWS // P
TB = SEQ // P
KN = 512
NKN = SEQ // KN
HALF = SEQ // 2
GRP = 128
NGRP = SEQ // GRP
NCAND = NGRP * 8 + 8
NEG = -(2.0 ** 100)
TIE = -(2.0 ** -100)
TAKEN = -3.0e38
SCALE = 1.0 / 16.0


class Tensors:
    pass


def sb(ctx, nc, name, shape, dt=FP32):
    return ctx.enter_context(nc.sbuf_tensor(name, shape, dt))


def psum(ctx, nc, name, shape, dt=FP32):
    return ctx.enter_context(nc.psum_tensor(name, shape, dt))


def sem(ctx, nc, name):
    return ctx.enter_context(nc.semaphore(name))


def f32(ap):
    return ap.bitcast(FP32)


def macaron_kernel(nc, d):
    d.kT = nc.dram_tensor("kT_scratch", [2, DC, P, ROWS], FP32).ap()
    d.qT = nc.dram_tensor("qT_scratch", [NT, P, 2, DC, P], FP32).ap()
    d.v = nc.dram_tensor("v_scratch", [2, P, NT, D], FP32).ap()
    d.ik = nc.dram_tensor("ik_scratch", [2, ID, ROWS], FP32).ap()
    d.iq = nc.dram_tensor("iq_scratch", [NT, 2, ID, IH, P], FP32).ap()
    d.iw = nc.dram_tensor("iw_scratch", [P, NT, IH], FP32).ap()
    d.x1 = nc.dram_tensor("x1_scratch", [ROWS, D], FP32).ap()
    d.x2 = nc.dram_tensor("x2_scratch", [ROWS, D], FP32).ap()

    with ExitStack() as outer:
        w = Tensors()
        w.w1h = sb(outer, nc, "w1h", [P, DC, F], FP32R)
        w.w1l = sb(outer, nc, "w1l", [P, DC, F], FP32R)
        w.w2h = sb(outer, nc, "w2h", [P, FC, D], FP32R)
        w.w2l = sb(outer, nc, "w2l", [P, FC, D], FP32R)
        w.wrh = sb(outer, nc, "wrh", [P, DC, E], FP32R)
        w.wrl = sb(outer, nc, "wrl", [P, DC, E], FP32R)
        w.b1c = sb(outer, nc, "b1c", [P, FC])
        w.b2b = sb(outer, nc, "b2b", [P, D])
        w.bvo = sb(outer, nc, "bvo", [P, D])
        w.ident = sb(outer, nc, "ident", [P, P])
        w.mhalf = sb(outer, nc, "mhalf", [P, RT])
        w.epsilon = sb(outer, nc, "epsilon", [P, RT])
        with ExitStack() as proj:
            w.wqkh = sb(proj, nc, "wqkh", [P, DC, 2 * D], FP32R)
            w.wqkl = sb(proj, nc, "wqkl", [P, DC, 2 * D], FP32R)
            w.wiqh = sb(proj, nc, "wiqh", [P, DC, D], FP32R)
            w.wiql = sb(proj, nc, "wiql", [P, DC, D], FP32R)
            w.wikh = sb(proj, nc, "wikh", [P, DC, ID], FP32R)
            w.wikl = sb(proj, nc, "wikl", [P, DC, ID], FP32R)
            w.wvwh = sb(proj, nc, "wvwh", [P, DC, D + IH], FP32R)
            w.wvwl = sb(proj, nc, "wvwl", [P, DC, D + IH], FP32R)
            w.bqkc = sb(proj, nc, "bqkc", [P, 2 * DC])
            w.biqc = sb(proj, nc, "biqc", [P, DC])
            w.bikc = sb(proj, nc, "bikc", [ID, 1])
            w.biwb = sb(proj, nc, "biwb", [P, IH])
            setup(nc, d, w)
            ffn_phase(nc, d, w, "a", d.x, d.x1)
        attention_phase(nc, d, w)
        ffn_phase(nc, d, w, "c", d.x2, d.out)


def setup(nc, d, w):
    with ExitStack() as ctx:
        w1f = sb(ctx, nc, "w1f", [P, DC, F])
        w2f = sb(ctx, nc, "w2f", [P, FC, D])
        wrf = sb(ctx, nc, "wrf", [P, DC, E])
        wqkf = sb(ctx, nc, "wqkf", [P, DC, 2 * D])
        wiqf = sb(ctx, nc, "wiqf", [P, DC, D])
        wikf = sb(ctx, nc, "wikf", [P, DC, ID])
        wvwf = sb(ctx, nc, "wvwf", [P, DC, D + IH])
        wvf = sb(ctx, nc, "wvf", [P, DC, D])
        wof = sb(ctx, nc, "wof", [P, DC, D])
        bvc = sb(ctx, nc, "bvc", [P, DC])
        bvm = sb(ctx, nc, "bvm", [P, DC, P])
        bob = sb(ctx, nc, "bob", [P, D])
        vo_ps = psum(ctx, nc, "vo_ps", [P, DC, D])
        bvo_ps = psum(ctx, nc, "bvo_ps", [P, D])
        vo_loaded = sem(ctx, nc, "vo_loaded")
        w_loaded = sem(ctx, nc, "w_loaded")
        c_loaded = sem(ctx, nc, "c_loaded")
        ident_set = sem(ctx, nc, "ident_set")
        bvm_set = sem(ctx, nc, "bvm_set")
        vo_done = sem(ctx, nc, "vo_done")
        vo_copied = sem(ctx, nc, "vo_copied")
        block = ctx.enter_context(nc.Block())

        def chunks(ap):
            return ap.rearrange("(c p) n -> p c n", p=P)

        weights = [(wqkf, d.wqkT), (wiqf, d.wiqT), (wikf, d.wikT), (w1f, d.w1), (w2f, d.w2), (wrf, d.wrT)]

        @block.sync
        def _(sp):
            sp.dma_start(wvf[:], chunks(d.wv)).then_inc(vo_loaded, 16)
            sp.dma_start(wof[:], chunks(d.woT)).then_inc(vo_loaded, 16)
            with nc.allow_non_contiguous_dma(reason="small weights and biases, once"):
                sp.dma_start(bvc[:], d.bv.rearrange("(c p) -> p c", p=P)).then_inc(vo_loaded, 16)
                sp.dma_start(wvwf[:, :, D:D + IH], chunks(d.wiwT)).then_inc(w_loaded, 16)
                for to, of in weights:
                    sp.dma_start(to[:], chunks(of)).then_inc(w_loaded, 16)
                for to, of in ((w.b1c, d.b1), (w.bqkc, d.bqk), (w.biqc, d.biq)):
                    sp.dma_start(to[:], of.rearrange("(c p) -> p c", p=P)).then_inc(c_loaded, 16)
                sp.dma_start(w.bikc[:], d.bik.unsqueeze(1)).then_inc(c_loaded, 16)
                sp.dma_start(w.biwb[:], d.biw.partition_broadcast(P)).then_inc(c_loaded, 16)
                sp.dma_start(w.b2b[:], d.b2.partition_broadcast(P)).then_inc(c_loaded, 16)
                sp.dma_start(bob[:], d.bo.partition_broadcast(P)).then_inc(c_loaded, 16)
            sp.wait_ge(c_loaded, 16 * 7)

        @block.gpsimd
        def _(pool):
            pool.memset(w.mhalf[:], -0.5)
            pool.memset(w.epsilon[:], EPS)
            pool.memset(w.ident[:], 0.0).then_inc(ident_set, 1)
            pool.wait_ge(ident_set, 1)
            pool.affine_select(out=w.ident[:], in_=w.ident[:], compare_op=ALU.not_equal, fill=1.0,
                               base=0, pattern=[[-1, P]], channel_multiplier=1)

        @block.tensor
        def _(pe):
            pe.wait_ge(vo_loaded, 48)
            for n in range(DC):
                for c in range(DC):
                    pe.matmul(vo_ps[:, n, :], wvf[:, c, n * P:(n + 1) * P], wof[:, c, :],
                              start=(c == 0), stop=(c == DC - 1)).then_inc(vo_done, 1)
            pe.wait_ge(bvm_set, DC)
            for c in range(DC):
                pe.matmul(bvo_ps[:], bvm[:, c, :], wof[:, c, :],
                          start=(c == 0), stop=(c == DC - 1)).then_inc(vo_done, 1)

        @block.vector
        def _(dve):
            dve.wait_ge(vo_loaded, 48)
            for c in range(DC):
                dve.tensor_copy(bvm[:, c, :], bvc[:, c:c + 1].to_broadcast([P, P])).then_inc(bvm_set, 1)
            dve.wait_ge(vo_done, DC * DC)
            for n in range(DC):
                dve.tensor_copy(wvwf[:, n, 0:D], vo_ps[:, n, :]).then_inc(vo_copied, 1)
            dve.wait_ge(vo_done, DC * DC + DC)
            dve.wait_ge(c_loaded, 16 * 7)
            dve.tensor_tensor(w.bvo[:], bvo_ps[:], bob[:], ALU.add)
            dve.wait_ge(w_loaded, 16 * (1 + len(weights)))
            dve.wait_ge(vo_copied, DC)
            parts = [(wvwf, w.wvwh, w.wvwl), (wqkf, w.wqkh, w.wqkl), (wiqf, w.wiqh, w.wiql),
                     (wikf, w.wikh, w.wikl), (w1f, w.w1h, w.w1l), (w2f, w.w2h, w.w2l), (wrf, w.wrh, w.wrl)]
            for whole, high, _ in parts:
                dve.tensor_copy(high[:], whole[:]).then_inc(vo_copied, 1)
            for n, (whole, high, low) in enumerate(parts):
                dve.wait_ge(vo_copied, DC + n + 1)
                dve.tensor_tensor(low[:], whole[:], f32(high[:]), ALU.subtract)


def ffn_phase(nc, d, w, phase, src, dst):
    with_proj = phase == "a"
    with ExitStack() as ctx:
        def buf(name, shape, dt=FP32):
            return sb(ctx, nc, name + phase, shape, dt)

        def bank(name, shape, dt=FP32):
            return psum(ctx, nc, name + phase, shape, dt)

        def count(name):
            return sem(ctx, nc, name + "_" + phase)

        xa = buf("xa", [P, RT, D])
        xr = buf("xr", [P, RT, D])
        xn = buf("xn", [P, RT, D])
        xTh = buf("xTh", [P, DC, GR], FP32R)
        xTl = buf("xTl", [P, DC, GR], FP32R)
        hf = buf("hf", [P, 2, GR])
        hh = buf("hh", [P, FC, GR], FP32R)
        hl = buf("hl", [P, FC, GR], FP32R)
        rs = buf("rs", [E, GR])
        re = buf("re", [P, RT, E])
        rx = buf("rx", [P, RT, E])
        rm = buf("rm", [P, RT])
        rsum = buf("rsum", [P, RT])
        rinv = buf("rinv", [P, RT])
        pr = buf("pr", [P, RT])
        st = buf("st", [P, RT, 6])
        mv = buf("mv", [P, RT, 2])
        ve = buf("ve", [P, RT])
        rstd = buf("rstd", [P, RT])
        table = buf("table", [P, 1])
        yb = buf("yb", [P, 2, D])
        xo = buf("xo", [P, RT, D])
        if with_proj:
            x1b = buf("x1b", [P, RT, D])
            xn2 = buf("xn2", [P, RT, D])
            yTh = buf("yTh", [P, DC, GR], FP32R)
            yTl = buf("yTl", [P, DC, GR], FP32R)
            st2 = buf("st2", [P, RT, 6])
            mv2 = buf("mv2", [P, RT, 2])
            ve2 = buf("ve2", [P, RT])
            rstd2 = buf("rstd2", [P, RT])
            cs = buf("cs", [P, 2, GR])
            raw = buf("raw", [P, 2, DC, GR])
            rc = buf("rc", [P, DC, GR])
            rsn = buf("rsn", [P, DC, GR])
            rot = buf("rot", [P, DC, GR])
            qh = buf("qh", [P, DC, GR], FP32R)
            ql = buf("ql", [P, DC, GR], FP32R)
            iqf = buf("iqf", [P, DC, GR])
            iqh = buf("iqh", [P, DC, GR], FP32R)
            iql = buf("iql", [P, DC, GR], FP32R)
            ikf = buf("ikf", [ID, GR])
            ikh = buf("ikh", [ID, GR], FP32R)
            ikl = buf("ikl", [ID, GR], FP32R)
            vh = buf("vh", [P, RT, D], FP32R)
            vl = buf("vl", [P, RT, D], FP32R)
            iw = buf("iw", [P, RT, IH])

        tp = bank("tp", [P, DC, GR])
        hp = bank("hp", [P, 2, GR])
        yp = bank("yp", [P, RT, D])
        rp = bank("rp", [P, GR])
        rt = bank("rt", [P, RT, E])
        yT = yp[:].rearrange("p r d -> p (r d)").rearrange("p (c n) -> p c n", c=DC)

        xa_loaded = count("xa_loaded")
        xr_loaded = count("xr_loaded")
        stats = count("stats")
        rstd_set = count("rstd_set")
        xn_set = count("xn_set")
        xT_done = count("xT_done")
        xTh_set = count("xTh_set")
        xTl_set = count("xTl_set")
        router_done = count("router_done")
        rs_set = count("rs_set")
        rt_done = count("rt_done")
        rx_set = count("rx_set")
        re_set = count("re_set")
        h_done = count("h_done")
        hf_set = count("hf_set")
        hh_set = count("hh_set")
        hl_set = count("hl_set")
        y_done = count("y_done")
        xo_set = count("xo_set")
        xo_stored = count("xo_stored")
        dve_step = count("dve_step")
        pool_step = count("pool_step")
        act_step = count("act_step")
        if with_proj:
            cs_loaded = count("cs_loaded")
            stats2 = count("stats2")
            rstd2_set = count("rstd2_set")
            xn2_set = count("xn2_set")
            yT_done = count("yT_done")
            yTh_set = count("yTh_set")
            yTl_set = count("yTl_set")
            x1b_set = count("x1b_set")
            p_done = count("p_done")
            p_read = count("p_read")
            raw_set = count("raw_set")
            rc_set = count("rc_set")
            rot_set = count("rot_set")
            qh_set = count("qh_set")
            ql_set = count("ql_set")
            iq_set = count("iq_set")
            iql_set = count("iql_set")
            ik_set = count("ik_set")
            ikl_set = count("ikl_set")
            vh_set = count("vh_set")
            q_stored = count("q_stored")
            iq_stored = count("iq_stored")
            v_stored = count("v_stored")
        block = ctx.enter_context(nc.Block())

        NP = 2 * DC + DC + 1 + RT

        def row_tiles(dram, row):
            return dram[bass.ds(row, GR), :].rearrange("(r p) d -> p r d", p=P)

        @block.sync
        def _(sp):
            def at(v):
                return v if isinstance(v, int) else sp.snap(v)

            def load_xa(g):
                row = at(g * GR)
                if not isinstance(g, int) or g > 0:
                    sp.wait_ge(xn_set, at(g * RT))
                sp.dma_start(xa[:], row_tiles(src, row)).then_inc(xa_loaded, 16)

            def load_xr(g):
                row = at(g * GR)
                if not isinstance(g, int) or g > 0:
                    sp.wait_ge(xo_set, at(g * RT))
                sp.dma_start(xr[:], row_tiles(src, row)).then_inc(xr_loaded, 16)

            def store_xo(g):
                row = at(g * GR)
                if with_proj:
                    sp.wait_ge(x1b_set, at(g + 1))
                    sp.dma_start(row_tiles(dst, row), x1b[:]).then_inc(xo_stored, 16)
                else:
                    sp.wait_ge(xo_set, at((g + 1) * RT))
                    sp.dma_start(row_tiles(dst, row), xo[:]).then_inc(xo_stored, 16)

            def load_cs(g):
                g = at(g)
                if not isinstance(g, int) or g > 0:
                    sp.wait_ge(rc_set, at(g * 4))
                sp.dma_start(cs[:], d.cs_t[bass.ds(g, 1), :, :, :].rearrange("g p t n -> (g p) t n")
                             ).then_inc(cs_loaded, 16)

            def store_rotated(g, which):
                row, tile = at(g * GR), at(g * RT)
                sp.wait_ge(ql_set, at(2 * g + which + 1))
                for part, t in enumerate((qh, ql)):
                    for c in range(DC):
                        if which == 0:
                            to = d.qT[bass.ds(tile, RT), :, part, c, :].rearrange("t p q -> p t q")
                            of = f32(t[:, c, :]).rearrange("p (t q) -> p t q", t=RT)
                        else:
                            to = d.kT[part, c, :, bass.ds(row, GR)]
                            of = f32(t[:, c, :])
                        sp.dma_start(to, of).then_inc(q_stored, 16)

            def store_proj(g):
                row, tile = at(g * GR), at(g * RT)
                sp.wait_ge(iql_set, at(g + 1))
                for part, t in enumerate((iqh, iql)):
                    for c in range(DC):
                        for a in range(2):
                            sp.dma_start(
                                d.iq[bass.ds(tile, RT), part, :, 2 * c + a, :].rearrange("t d q -> d t q"),
                                f32(t[a * ID:(a + 1) * ID, c, :]).rearrange("d (t q) -> d t q", t=RT),
                            ).then_inc(iq_stored, 16)
                sp.wait_ge(ikl_set, at(g + 1))
                for part, t in enumerate((ikh, ikl)):
                    sp.dma_start(d.ik[part, :, bass.ds(row, GR)], f32(t[:])).then_inc(iq_stored, 16)
                sp.wait_ge(p_read, at((g + 1) * NP))
                for part, t in enumerate((vh, vl)):
                    sp.dma_start(d.v[part, :, bass.ds(tile, RT), :], f32(t[:])).then_inc(v_stored, 16)
                sp.dma_start(d.iw[:, bass.ds(tile, RT), :], iw[:]).then_inc(v_stored, 16)

            def body(g, before=2, more=2):
                if more > 1:
                    load_xa(g + 2)
                if with_proj and before > 1:
                    store_rotated(g - 2, 0)
                    load_cs(g - 1)
                if more > 0:
                    load_xr(g + 1)
                store_xo(g)
                if with_proj and before > 1:
                    store_rotated(g - 2, 1)
                if with_proj and before > 0:
                    store_proj(g - 1)

            load_xa(0)
            load_xr(0)
            if with_proj:
                load_cs(0)
            load_xa(1)
            body(0, before=0)
            body(1, before=1)
            with sp.Fori(2, NG - 2) as g:
                body(g)
            body(NG - 2, more=1)
            body(NG - 1, more=0)
            if with_proj:
                store_rotated(NG - 2, 0)
                load_cs(NG - 1)
                store_rotated(NG - 2, 1)
                store_proj(NG - 1)
                store_rotated(NG - 1, 0)
                store_rotated(NG - 1, 1)
                sp.wait_ge(q_stored, NG * 4 * DC * 16)
                sp.wait_ge(iq_stored, NG * (4 * DC + 2) * 16)
                sp.wait_ge(v_stored, NG * 3 * 16)
            sp.wait_ge(xo_stored, NG * 16)

        @block.tensor
        def _(pe):
            def transposes(g, rows, ready, to, done):
                for r in range(RT):
                    pe.wait_ge(ready, g * RT + r + 1)
                    for c in range(DC):
                        ins = pe.transpose(to[:, c, r * P:(r + 1) * P], rows[:, r, c * P:(c + 1) * P], w.ident[:])
                        if r == RT - 1:
                            ins.then_inc(done, 1)

            def three(to, lhs, rhs, start, stop):
                (lh, ll), (rh, rl) = lhs, rhs
                pe.matmul(to, lh, rh, start=start, stop=False)
                pe.matmul(to, ll, rh, start=False, stop=False)
                return pe.matmul(to, lh, rl, start=False, stop=stop)

            def ffn_up(g):
                pe.wait_ge(xTl_set, (g + 1) * DC)
                if not isinstance(g, int) or g > 0:
                    pe.wait_ge(rs_set, g)
                for c in range(DC):
                    ins = three(rp[0:E, :], (w.wrh[:, c, :], w.wrl[:, c, :]), (xTh[:, c, :], xTl[:, c, :]),
                                c == 0, c == DC - 1)
                ins.then_inc(router_done, 1)
                for f in range(FC):
                    if not isinstance(g, int) or g > 0 or f >= 2:
                        pe.wait_ge(hf_set, g * FC + f - 1)
                    if with_proj and f < 2 and (not isinstance(g, int) or g > 1):
                        pe.wait_ge(p_read, (g - 1) * NP)
                    if f == 2:
                        pe.wait_ge(rs_set, g + 1)
                        if not isinstance(g, int) or g > 0:
                            pe.wait_ge(rx_set, g)
                    fs = slice(f * P, (f + 1) * P)
                    for c in range(DC):
                        ins = three(hp[:, f % 2, :], (w.w1h[:, c, fs], w.w1l[:, c, fs]),
                                    (xTh[:, c, :], xTl[:, c, :]), c == 0, c == DC - 1)
                    ins.then_inc(h_done, 1)
                    if f == 2:
                        for r in range(RT):
                            ins = pe.transpose(rt[:, r, :], rs[:, r * P:(r + 1) * P], w.ident[0:E, 0:E])
                        ins.then_inc(rt_done, 1)

            def ffn_down(g):
                if not isinstance(g, int) or g > 0:
                    pe.wait_ge(xo_set, g * RT)
                for r in range(RT):
                    rs_ = slice(r * P, (r + 1) * P)
                    for f in range(FC):
                        if r == 0:
                            pe.wait_ge(hl_set, g * FC + f + 1)
                        ins = three(yp[:, r, :], (hh[:, f, rs_], hl[:, f, rs_]), (w.w2h[:, f, :], w.w2l[:, f, :]),
                                    f == 0, f == FC - 1)
                    ins.then_inc(y_done, 1)

            def project(g):
                pe.wait_ge(yTl_set, (g + 1) * DC)
                n = 0

                def free(n):
                    if n >= 2:
                        pe.wait_ge(p_read, g * NP + n - 1)
                for lo, m, wh, wl in ([(c * P, P, w.wqkh, w.wqkl) for c in range(2 * DC)]
                                      + [(c * P, P, w.wiqh, w.wiql) for c in range(DC)]
                                      + [(0, ID, w.wikh, w.wikl)]):
                    free(n)
                    for c in range(DC):
                        ins = three(hp[0:m, n % 2, :], (wh[:, c, lo:lo + m], wl[:, c, lo:lo + m]),
                                    (yTh[:, c, :], yTl[:, c, :]), c == 0, c == DC - 1)
                    ins.then_inc(p_done, 1)
                    n += 1
                for r in range(RT):
                    free(n)
                    rs_ = slice(r * P, (r + 1) * P)
                    for c in range(DC):
                        ins = three(hp[:, n % 2, 0:D + IH], (yTh[:, c, rs_], yTl[:, c, rs_]),
                                    (w.wvwh[:, c, :], w.wvwl[:, c, :]), c == 0, c == DC - 1)
                    ins.then_inc(p_done, 1)
                    n += 1

            def body(g, first=False, last=False):
                if with_proj and not first:
                    pe.wait_ge(xo_set, g * RT)
                    transposes(g - 1, xn2, xn2_set, yT, yT_done)
                ffn_up(g)
                if not last:
                    transposes(g + 1, xn, xn_set, tp, xT_done)
                if with_proj and not first:
                    pe.wait_ge(yTl_set, g * DC)
                ffn_down(g)
                if with_proj and not first:
                    pe.wait_ge(hf_set, (g + 1) * FC)
                    project(g - 1)

            transposes(0, xn, xn_set, tp, xT_done)
            body(0, first=True)
            body(1)
            with pe.Fori(2, NG - 1) as g:
                body(g)
            body(NG - 1, last=True)
            if with_proj:
                pe.wait_ge(xo_set, NG * RT)
                transposes(NG - 1, xn2, xn2_set, yT, yT_done)
                pe.wait_ge(p_read, (NG - 1) * NP)
                project(NG - 1)

        @block.scalar
        def _(act):
            def split_high(g, bank, done, to, to_set):
                for c in range(DC):
                    act.wait_ge(done, g * DC + c + 1)
                    act.activation(to[:, c, :], bank[:, c, :], ACT.Copy).then_inc(to_set, 1)

            def ffn(g, last=False):
                act.activation(table[:], w.epsilon[:, 0:1], ACT.Gelu)
                act.wait_ge(router_done, g + 1)
                act.activation(rs[:], rp[0:E, :], ACT.Copy).then_inc(rs_set, 1)
                for f in range(FC):
                    act.wait_ge(h_done, g * FC + f + 1)
                    if not isinstance(g, int) or g > 0 or f >= 2:
                        act.wait_ge(hl_set, g * FC + f - 1)
                    act.activation(hf[:, f % 2, :], hp[:, f % 2, :], ACT.Gelu,
                                   bias=w.b1c[:, f:f + 1]).then_inc(hf_set, 1)
                if not last:
                    split_high(g + 1, tp, xT_done, xTh, xTh_set)
                act.wait_ge(rx_set, g + 1)
                act.activation(re[:], rx[:], ACT.Exp).then_inc(re_set, 1)

            def project(g):
                for n in range(2 * DC):
                    act.wait_ge(p_done, g * NP + n + 1)
                    if n % DC == 0 and (not isinstance(g, int) or g > 0):
                        act.wait_ge(rc_set, 4 * g - 2 + n)
                    act.activation(raw[:, n // DC, n % DC, :], hp[:, n % 2, :], ACT.Identity,
                                   bias=w.bqkc[:, n:n + 1]).then_inc(p_read, 1)
                for c in range(DC):
                    act.wait_ge(p_done, g * NP + 2 * DC + c + 1)
                    if c == 0 and (not isinstance(g, int) or g > 0):
                        act.wait_ge(iql_set, g)
                        act.wait_ge(iq_stored, g * (4 * DC + 2) * 16)
                    act.activation(iqh[:, c, :], hp[:, c % 2, :], ACT.Identity,
                                   bias=w.biqc[:, c:c + 1]).then_inc(iq_set, 1)
                    act.activation(iqf[:, c, :], hp[:, c % 2, :], ACT.Identity,
                                   bias=w.biqc[:, c:c + 1]).then_inc(p_read, 1)
                act.wait_ge(p_done, g * NP + 3 * DC + 1)
                if not isinstance(g, int) or g > 0:
                    act.wait_ge(ikl_set, g)
                act.activation(ikh[:], hp[0:ID, 0, :], ACT.Identity, bias=w.bikc[:]).then_inc(ik_set, 1)
                act.activation(ikf[:], hp[0:ID, 0, :], ACT.Identity, bias=w.bikc[:]).then_inc(p_read, 1)
                for r in range(RT):
                    act.wait_ge(p_done, g * NP + 3 * DC + r + 2)
                    if r == 0 and (not isinstance(g, int) or g > 0):
                        act.wait_ge(v_stored, g * 3 * 16)
                    act.activation(vh[:, r, :], hp[:, (r + 1) % 2, 0:D], ACT.Copy).then_inc(vh_set, 1)

            def body(g, first=False, last=False):
                if with_proj and not first:
                    split_high(g - 1, yT, yT_done, yTh, yTh_set)
                ffn(g, last)
                if with_proj and not first:
                    project(g - 1)

            split_high(0, tp, xT_done, xTh, xTh_set)
            body(0, first=True)
            body(1)
            with act.Fori(2, NG - 1) as g:
                body(g)
            body(NG - 1, last=True)
            if with_proj:
                split_high(NG - 1, yT, yT_done, yTh, yTh_set)
                project(NG - 1)

        @block.gpsimd
        def _(pool):
            def inverse_std(g, stats, mv, ve, rstd, rstd_set):
                pool.wait_ge(stats, (g + 1) * RT)
                pool.tensor_tensor(ve[:], mv[:, :, 1], w.epsilon[:], ALU.add).then_inc(pool_step, 1)
                pool.wait_ge(pool_step, 1)
                pool.tensor_tensor(rstd[:], ve[:], w.mhalf[:], ALU.pow).then_inc(rstd_set, 1)
                pool.sem_clear(pool_step)

            def rotate(g, which):
                pool.wait_ge(p_read, g * NP + DC * (which + 1))
                if which == 0:
                    pool.wait_ge(cs_loaded, (g + 1) * 16)
                if not isinstance(g, int) or g > 0 or which > 0:
                    pool.wait_ge(rot_set, 4 * g + 2 * which)
                for t, n in ((rc, 0), (rsn, 1)):
                    pool.tensor_tensor(t[:], raw[:, which, :, :], cs[:, n:n + 1, :].to_broadcast([P, DC, GR]),
                                       ALU.mult).then_inc(rc_set, 1)

            def body(g, before=2, last=False):
                if with_proj and before > 1:
                    rotate(g - 2, 0)
                if not last:
                    inverse_std(g + 1, stats, mv, ve, rstd, rstd_set)
                if with_proj:
                    if before > 1:
                        rotate(g - 2, 1)
                    inverse_std(g, stats2, mv2, ve2, rstd2, rstd2_set)
                    if before > 0:
                        pool.wait_ge(xo_stored, g * 16)
                    pool.wait_ge(xo_set, (g + 1) * RT)
                    pool.tensor_tensor(x1b[:], xo[:], w.bvo[:].unsqueeze(1).to_broadcast([P, RT, D]),
                                       ALU.add).then_inc(x1b_set, 1)

            inverse_std(0, stats, mv, ve, rstd, rstd_set)
            body(0, before=0)
            body(1, before=1)
            with pool.Fori(2, NG - 1) as g:
                body(g)
            body(NG - 1, last=True)
            if with_proj:
                for g in (NG - 2, NG - 1):
                    rotate(g, 0)
                    rotate(g, 1)

        @block.vector
        def _(dve):
            steps = [0]

            def step(ins):
                steps[0] += 1
                ins.then_inc(dve_step, 1)
                return steps[0]

            def clear_steps():
                dve.wait_ge(dve_step, steps[0])
                dve.sem_clear(dve_step)
                steps[0] = 0

            def row_stats(g, rows, st, mv, stats_sem):
                last = [step(dve.bn_stats(st[:, r, :], rows[:, r, :])) for r in range(RT)]
                for r in range(RT):
                    dve.wait_ge(dve_step, last[r])
                    dve.bn_aggr(mv[:, r, :], st[:, r, :]).then_inc(stats_sem, 1)

            def normalise(g, rows, mv, rstd, rstd_set, stats_sem, to, to_set):
                dve.wait_ge(rstd_set, g + 1)
                dve.wait_ge(stats_sem, (g + 1) * RT)
                for r in range(RT):
                    dve.tensor_scalar(to[:, r, :], rows[:, r, :], mv[:, r, 0:1], rstd[:, r:r + 1],
                                      ALU.subtract, ALU.mult).then_inc(to_set, 1)

            def split_low(g, bank, high, high_set, low, low_set):
                for c in range(DC):
                    dve.wait_ge(high_set, g * DC + c + 1)
                    dve.tensor_tensor(low[:, c, :], bank[:, c, :], f32(high[:, c, :]),
                                      ALU.subtract).then_inc(low_set, 1)

            def split_hidden(g, f):
                dve.wait_ge(hf_set, g * FC + f + 1)
                if f == 0 and (not isinstance(g, int) or g > 0):
                    dve.wait_ge(y_done, g * RT)
                dve.tensor_copy(hh[:, f, :], hf[:, f % 2, :]).then_inc(hh_set, 1)
                dve.wait_ge(hh_set, g * FC + f + 1)
                dve.tensor_tensor(hl[:, f, :], hf[:, f % 2, :], f32(hh[:, f, :]), ALU.subtract).then_inc(hl_set, 1)

            def router_max(g):
                dve.wait_ge(rt_done, g + 1)
                n = step(dve.reduce_max(rm[:], rt[:], AX.X))
                dve.wait_ge(dve_step, n)
                dve.tensor_tensor(rx[:], rt[:], rm[:].unsqueeze(2).to_broadcast([P, RT, E]),
                                  ALU.subtract).then_inc(rx_set, 1)

            def router_prob(g):
                dve.wait_ge(re_set, g + 1)
                n = step(dve.reduce_sum(rsum[:], re[:], AX.X))
                dve.wait_ge(dve_step, n)
                n = step(dve.reciprocal(rinv[:], rsum[:]))
                dve.wait_ge(dve_step, n)
                return step(dve.scalar_tensor_tensor(pr[:], re[:, :, E - 1], 0.5, rinv[:], ALU.mult, ALU.mult))

            def residual(g, prob_step):
                dve.wait_ge(xr_loaded, (g + 1) * 16)
                if not with_proj and (not isinstance(g, int) or g > 0):
                    dve.wait_ge(xo_stored, g * 16)
                if with_proj and (not isinstance(g, int) or g > 0):
                    dve.wait_ge(x1b_set, g)
                dve.wait_ge(dve_step, prob_step)
                for r in range(RT):
                    dve.wait_ge(y_done, g * RT + r // 2 * 2 + 2)
                    n = step(dve.tensor_tensor(yb[:, r % 2, :], yp[:, r, :], w.b2b[:], ALU.add))
                    dve.wait_ge(dve_step, n)
                    dve.scalar_tensor_tensor(xo[:, r, :], yb[:, r % 2, :], pr[:, r:r + 1], xr[:, r, :],
                                             ALU.mult, ALU.add).then_inc(xo_set, 1)

            def rotated(g, which):
                dve.wait_ge(rc_set, 4 * g + 2 * which + 2)
                if not isinstance(g, int) or g > 0 or which > 0:
                    dve.wait_ge(q_stored, (2 * g + which) * 2 * DC * 16)
                dve.tensor_tensor(rot[:, 0, :], rc[:, 0, :], rsn[:, 1, :], ALU.subtract).then_inc(rot_set, 1)
                dve.tensor_tensor(rot[:, 1, :], rsn[:, 0, :], rc[:, 1, :], ALU.add).then_inc(rot_set, 1)
                dve.wait_ge(rot_set, 4 * g + 2 * which + 2)
                dve.tensor_copy(qh[:], rot[:]).then_inc(qh_set, 1)
                dve.wait_ge(qh_set, 2 * g + which + 1)
                dve.tensor_tensor(ql[:], rot[:], f32(qh[:]), ALU.subtract).then_inc(ql_set, 1)

            def project(g):
                dve.wait_ge(iq_set, (g + 1) * DC)
                dve.wait_ge(p_read, g * NP + 3 * DC)
                if not isinstance(g, int) or g > 0:
                    dve.wait_ge(iq_stored, g * (4 * DC + 2) * 16)
                dve.tensor_tensor(iql[:], iqf[:], f32(iqh[:]), ALU.subtract).then_inc(iql_set, 1)
                dve.wait_ge(ik_set, g + 1)
                dve.wait_ge(p_read, g * NP + 3 * DC + 1)
                dve.tensor_tensor(ikl[:], ikf[:], f32(ikh[:]), ALU.subtract).then_inc(ikl_set, 1)
                if not isinstance(g, int) or g > 0:
                    dve.wait_ge(v_stored, g * 3 * 16)
                for r in range(RT):
                    bank = hp[:, (r + 1) % 2, :]
                    dve.wait_ge(vh_set, g * RT + r + 1)
                    dve.tensor_tensor(iw[:, r, :], bank[:, D:D + IH], w.biwb[:], ALU.add)
                    dve.tensor_tensor(vl[:, r, :], bank[:, 0:D], f32(vh[:, r, :]), ALU.subtract).then_inc(p_read, 1)

            def body(g, before=2, last=False):
                if with_proj and before > 0:
                    split_low(g - 1, yT, yTh, yTh_set, yTl, yTl_set)
                for f in range(FC):
                    split_hidden(g, f)
                    if f == 1 and not last:
                        dve.wait_ge(xa_loaded, (g + 2) * 16)
                        row_stats(g + 1, xa, st, mv, stats)
                    if f == 4:
                        router_max(g)
                    if f == 5 and not last:
                        normalise(g + 1, xa, mv, rstd, rstd_set, stats, xn, xn_set)
                if not last:
                    split_low(g + 1, tp, xTh, xTh_set, xTl, xTl_set)
                n = router_prob(g)
                if with_proj and before > 1:
                    rotated(g - 2, 0)
                residual(g, n)
                if with_proj:
                    dve.wait_ge(xo_set, (g + 1) * RT)
                    row_stats(g, xo, st2, mv2, stats2)
                    if before > 1:
                        rotated(g - 2, 1)
                    normalise(g, xo, mv2, rstd2, rstd2_set, stats2, xn2, xn2_set)
                    if before > 0:
                        project(g - 1)
                clear_steps()

            dve.wait_ge(xa_loaded, 16)
            row_stats(0, xa, st, mv, stats)
            normalise(0, xa, mv, rstd, rstd_set, stats, xn, xn_set)
            split_low(0, tp, xTh, xTh_set, xTl, xTl_set)
            clear_steps()
            body(0, before=0)
            body(1, before=1)
            with dve.Fori(2, NG - 1) as g:
                body(g)
            body(NG - 1, last=True)
            if with_proj:
                rotated(NG - 2, 0)
                split_low(NG - 1, yT, yTh, yTh_set, yTl, yTl_set)
                rotated(NG - 2, 1)
                project(NG - 1)
                rotated(NG - 1, 0)
                rotated(NG - 1, 1)


def attention_phase(nc, d, w):
    UNITS = [(3, 0), (2, 0), (1, 0), (3, 1), (2, 1), (1, 1), (0, 0), (0, 1)]
    NU = len(UNITS)
    ALL_OUT = NEG * P * (SEQ - TOPK)
    with ExitStack() as ctx:
        def buf(name, shape, dt=FP32):
            return sb(ctx, nc, name, shape, dt)

        def bank(name, shape, dt=FP32):
            return psum(ctx, nc, name, shape, dt)

        def count(name):
            return sem(ctx, nc, "att_" + name)

        kT = buf("kT", [P, 2, DC, SEQ], FP32R)
        v = buf("v", [P, 2, TB, D], FP32R)
        ik = buf("ik", [P, SEQ], FP32R)
        iq = buf("iq", [P, 2, IH, P], FP32R)
        qT = buf("qT", [P, 2, DC, P], FP32R)
        iwp = buf("iwp", [P, IH])
        iwd = buf("iwd", [P, IH])
        x1t = buf("x1t", [P, D])
        x2t = buf("x2t", [P, D])
        relus = buf("relus", [P, IH, SEQ])
        u = buf("u", [P, SEQ])
        tie = buf("tie", [P, HALF])
        tie_i = buf("tie_i", [P, HALF], I32)
        sc = buf("sc", [P, 2, SEQ])
        rest = buf("rest", [P, SEQ])
        cand = buf("cand", [P, NCAND])
        best = buf("best", [P, 8])
        redo_best = buf("redo_best", [P, 8])
        bias = buf("bias", [P, SEQ], BF16)
        cnt = buf("cnt", [P, 1])
        ones = buf("ones", [P, 1])
        gate = buf("gate", [P, 2])
        dve_gate = buf("dve_gate", [1, NKN + 1])
        redo = buf("redo", [1, 1], I32)
        pr = buf("pr", [P, SEQ])
        mx = buf("mx", [P, NKN])
        nm = buf("nm", [P, 1])
        rsum = buf("rsum_t", [P, 1])
        rinv = buf("rinv_t", [P, 1])
        pTh = buf("pTh", [P, 2, KN], FP32R)
        pTl = buf("pTl", [P, 2, KN], FP32R)

        zp = bank("zp", [P, 2, HALF])
        lp = bank("lp", [P, 2, KN])
        pt = bank("pt", [P, KN])
        op = bank("op", [P, KN])

        ik_loaded = count("ik_loaded")
        k_loaded = [count(f"k{n}_loaded") for n in range(NKN)]
        v_loaded = [count(f"v{n}_loaded") for n in range(NKN)]
        iq_loaded = count("iq_loaded")
        iwp_loaded = count("iwp_loaded")
        iwd_loaded = count("iwd_loaded")
        q_loaded = count("q_loaded")
        x1_loaded = count("x1_loaded")
        x2_stored = count("x2_stored")
        z_done = count("z_done")
        relu_set = count("relu_set")
        weighted = count("weighted")
        u_set = count("u_set")
        s_set = count("s_set")
        bias_set = count("bias_set")
        cnt_set = count("cnt_set")
        check_done = count("check_done")
        l_done = count("l_done")
        m_set = count("m_set")
        nm_set = count("nm_set")
        p_set = count("p_set")
        pt_done = count("pt_done")
        pth_set = count("pth_set")
        ptl_set = count("ptl_set")
        o_done = count("o_done")
        x2_set = count("x2_set")
        dve_step = count("dve_step")
        redo_step = count("redo_step")
        pool_step = count("pool_step")
        const_set = count("const_set")
        block = ctx.enter_context(nc.Block())

        @block.sync
        def _(sp):
            def at(v):
                return v if isinstance(v, int) else sp.snap(v)

            def positive(g):
                return not isinstance(g, int) or g > 0

            def load_ik(b):
                row = at(b * SEQ)
                if positive(b):
                    sp.wait_ge(z_done, at(b * TB * NU))
                for part in range(2):
                    sp.dma_start(f32(ik[part * ID:(part + 1) * ID, :]),
                                 d.ik[part, :, bass.ds(row, SEQ)]).then_inc(ik_loaded, 16)

            def load_k(b, quarters):
                for n in quarters:
                    row = at(b * SEQ + n * KN)
                    if positive(b):
                        sp.wait_ge(l_done, at(b * TB * NKN - NKN + n + 1))
                    for part in range(2):
                        for c in range(DC):
                            sp.dma_start(f32(kT[:, part, c, n * KN:(n + 1) * KN]),
                                         d.kT[part, c, :, bass.ds(row, KN)]).then_inc(k_loaded[n], 16)

            def load_v(b):
                for n in range(NKN):
                    row = at(b * TB + n * 4)
                    if positive(b):
                        sp.wait_ge(o_done, at(b * TB * NKN - NKN + n + 1))
                    for part in range(2):
                        sp.dma_start(f32(v[:, part, n * 4:(n + 1) * 4, :]),
                                     d.v[part, :, bass.ds(row, 4), :]).then_inc(v_loaded[n], 16)

            def load_iq(i):
                i = at(i)
                if positive(i):
                    sp.wait_ge(z_done, at(i * NU))
                for a in range(2):
                    sp.dma_start(f32(iq[a * ID:(a + 1) * ID, :, :, :]),
                                 d.iq[bass.ds(i, 1), :, :, :, :].rearrange("t part d h q -> (t d) part h q")
                                 ).then_inc(iq_loaded, 16)

            def load_iwp(i):
                i = at(i)
                if positive(i):
                    sp.wait_ge(u_set, at(i * 2))
                sp.dma_start(iwp[:], d.iw[:, bass.ds(i, 1), :].rearrange("p t h -> p (t h)")).then_inc(iwp_loaded, 16)

            def load_iwd(i):
                i = at(i)
                if positive(i):
                    sp.wait_ge(s_set, at(i * 2))
                sp.dma_start(iwd[:], d.iw[:, bass.ds(i, 1), :].rearrange("p t h -> p (t h)")).then_inc(iwd_loaded, 16)

            def load_q(i):
                i = at(i)
                if positive(i):
                    sp.wait_ge(l_done, at(i * NKN))
                sp.dma_start(f32(qT[:]), d.qT[bass.ds(i, 1), :, :, :, :].rearrange("t p a c q -> (t p) a c q")
                             ).then_inc(q_loaded, 16)

            def load_x1(i):
                row = at(i * P)
                if positive(i):
                    sp.wait_ge(x2_set, at(i))
                sp.dma_start(x1t[:], d.x1[bass.ds(row, P), :]).then_inc(x1_loaded, 16)

            def store_x2(i):
                row = at(i * P)
                sp.wait_ge(x2_set, at(i + 1))
                sp.dma_start(d.x2[bass.ds(row, P), :], x2t[:]).then_inc(x2_stored, 16)

            def tile(i, b, j, started=2, more=2):
                if j == 0 and started > 0:
                    load_k(b, (0, 1))
                if started > 0:
                    load_x1(i - 1)
                if started > 1:
                    store_x2(i - 2)
                if more > 0:
                    load_iwd(i + 1)
                if more > 1:
                    if j == TB - 2:
                        load_ik(b + 1)
                    load_iq(i + 2)
                if started > 0:
                    if j == 0:
                        load_k(b, (2, 3))
                    load_q(i)
                if more > 1:
                    load_iwp(i + 2)
                if j == 0 and started > 0:
                    load_v(b)

            def batch(b, first=False, last=False):
                tile(b * TB, b, 0, started=0 if first else 2)
                tile(b * TB + 1, b, 1, started=1 if first else 2)
                with sp.Fori(2, TB - 2) as j:
                    tile(b * TB + j, b, None)
                tile(b * TB + TB - 2, b, TB - 2, more=1 if last else 2)
                tile(b * TB + TB - 1, b, None, more=0 if last else 2)

            load_ik(0)
            load_iq(0)
            load_iwp(0)
            load_iwd(0)
            load_q(0)
            load_k(0, range(NKN))
            load_v(0)
            load_iq(1)
            load_iwp(1)
            batch(0, first=True)
            with sp.Fori(1, BATCH - 1) as b:
                batch(b)
            batch(BATCH - 1, last=True)
            load_x1(NT - 1)
            store_x2(NT - 2)
            store_x2(NT - 1)
            sp.wait_ge(x2_stored, NT * 16)

        @block.tensor
        def _(pe):
            def three(to, lhs, rhs, start, stop):
                (lh, ll), (rh, rl) = lhs, rhs
                pe.matmul(to, lh, rh, start=start, stop=False)
                pe.matmul(to, ll, rh, start=False, stop=False)
                return pe.matmul(to, lh, rl, start=False, stop=stop)

            def score_unit(i, n):
                head, half = UNITS[n]
                if n == 0:
                    pe.wait_ge(iq_loaded, (i + 1) * 32)
                    pe.wait_ge(ik_loaded, (i // TB + 1) * 32)
                if not isinstance(i, int) or i > 0 or n > 1:
                    pe.wait_ge(relu_set, i * NU + n - 1)
                for k in range(2):
                    keys = slice(half * HALF + k * KN, half * HALF + (k + 1) * KN)
                    for part in range(2):
                        ins = pe.matmul(zp[:, n % 2, k * KN:(k + 1) * KN], iq[:, part, head, :], ik[:, keys],
                                        start=(part == 0), stop=(part == 1))
                ins.then_inc(z_done, 1)

            def transposes(i, c):
                if c == 0:
                    pe.wait_ge(p_set, i + 1)
                if not isinstance(i, int) or i > 0 or c > 0:
                    pe.wait_ge(ptl_set, i * NKN + c)
                for k in range(4):
                    keys = slice(c * KN + k * P, c * KN + (k + 1) * P)
                    ins = pe.transpose(pt[:, k * P:(k + 1) * P], pr[:, keys], w.ident[:])
                ins.then_inc(pt_done, 1)

            def values(i, c):
                pe.wait_ge(v_loaded[c], (i // TB + 1) * 32)
                if c == 0 and (not isinstance(i, int) or i > 0):
                    pe.wait_ge(x2_set, i)
                pe.wait_ge(ptl_set, i * NKN + c + 1)
                for k in range(4):
                    kc = c * 4 + k
                    ks = slice(k * P, (k + 1) * P)
                    ins = three(op[:, 0:D], (pTh[:, c % 2, ks], pTl[:, c % 2, ks]), (v[:, 0, kc, :], v[:, 1, kc, :]),
                                kc == 0, kc == TB - 1)
                ins.then_inc(o_done, 1)

            def logits(i, banks):
                pe.wait_ge(q_loaded, (i + 1) * 16)
                for n in banks:
                    pe.wait_ge(k_loaded[n], (i // TB + 1) * 64)
                    if not isinstance(i, int) or i > 0 or n > 1:
                        pe.wait_ge(m_set, i * NKN + n - 1)
                    keys = slice(n * KN, (n + 1) * KN)
                    for c in range(DC):
                        ins = three(lp[:, n % 2, :], (qT[:, 0, c, :], qT[:, 1, c, :]),
                                    (kT[:, 0, c, keys], kT[:, 1, c, keys]), c == 0, c == DC - 1)
                    ins.then_inc(l_done, 1)

            def check(i):
                pe.wait_ge(cnt_set, i + 1)
                if not isinstance(i, int) or i > 0:
                    pe.wait_ge(x2_set, i)
                pe.matmul(op[0:1, KN - 1:KN], cnt[:], ones[:], start=True, stop=True).then_inc(check_done, 1)

            def tile(i, first=False, more=2):
                def units(ns):
                    for n in ns:
                        if more > 1:
                            score_unit(i + 1, n)

                units((0,))
                if not first:
                    check(i - 1)
                units((1, 2, 3))
                if not first:
                    logits(i - 1, (2, 3))
                units((4, 5))
                if not first:
                    transposes(i - 1, 0)
                units((6,))
                if not first:
                    transposes(i - 1, 1)
                    values(i - 1, 0)
                units((7,))
                if not first:
                    for c in range(2, NKN):
                        transposes(i - 1, c)
                        values(i - 1, c - 1)
                    values(i - 1, NKN - 1)
                if more > 0:
                    logits(i, (0, 1))

            pe.wait_ge(const_set, 5)
            for n in range(NU):
                score_unit(0, n)
            tile(0, first=True)
            tile(1)
            with pe.Fori(2, NT - 1) as i:
                tile(i)
            tile(NT - 1, more=1)
            tile(NT, more=0)

        @block.scalar
        def _(act):
            def relu(i, n):
                head, half = UNITS[n]
                keys = slice(half * HALF, (half + 1) * HALF)
                act.wait_ge(z_done, i * NU + n + 1)
                if not isinstance(i, int) or i > 0:
                    if head > 0:
                        act.wait_ge(u_set, (i - 1) * 2 + half + 1)
                    else:
                        act.wait_ge(s_set, (i - 1) * 2 + half + 1)
                act.activation(relus[:, head, keys], zp[:, n % 2, :], ACT.Relu).then_inc(relu_set, 1)
                if head == 1:
                    act.wait_ge(iwp_loaded, (i + 1) * 16)
                    act.wait_ge(relu_set, i * NU + n + 1)
                    act.activation(relus[:, 1, keys], relus[:, 1, keys], ACT.Copy,
                                   scale=iwp[:, 1:2]).then_inc(weighted, 1)

            def high(i, c):
                act.wait_ge(pt_done, i * NKN + c + 1)
                if not isinstance(i, int) or i > 0 or c >= 2:
                    act.wait_ge(o_done, i * NKN + c - 1)
                act.activation(pTh[:, c % 2, :], pt[:], ACT.Copy).then_inc(pth_set, 1)

            def exponentials(i):
                act.wait_ge(nm_set, i + 1)
                act.activation(pr[:], pr[:], ACT.Exp, bias=nm[:], accum_out=rsum[:]).then_inc(p_set, 1)

            def left_out(i):
                act.wait_ge(bias_set, i + 1)
                act.activation(bias[:], bias[:], ACT.Copy, accum_out=cnt[:]).then_inc(cnt_set, 1)

            def tile(i, first=False, more=2):
                if not first:
                    left_out(i - 1)
                if more > 1:
                    for n in range(5):
                        relu(i + 1, n)
                if not first:
                    exponentials(i - 1)
                for c in range(NKN):
                    if not first:
                        high(i - 1, c)
                    if c > 0 and more > 1:
                        relu(i + 1, 4 + c)

            for n in range(NU):
                relu(0, n)
            tile(0, first=True)
            tile(1)
            with act.Fori(2, NT - 1) as i:
                tile(i)
            tile(NT - 1, more=1)
            tile(NT, more=0)

        @block.gpsimd
        def _(pool):
            pool.memset(ones[:], 1.0).then_inc(const_set, 1)
            pool.iota(tie_i[:], [[1, HALF]], base=0, channel_multiplier=0).then_inc(const_set, 1)
            pool.wait_ge(const_set, 2)
            pool.tensor_scalar(tie[:], tie_i[:], TIE, 0.0, ALU.mult, ALU.add).then_inc(const_set, 3)

            def weigh(i):
                pool.wait_ge(iwp_loaded, (i + 1) * 16)
                n = 0
                for half in range(2):
                    keys = slice(half * HALF, (half + 1) * HALF)
                    pool.wait_ge(relu_set, i * NU + 3 * half + 2)
                    if not isinstance(i, int) or i > 0:
                        pool.wait_ge(s_set, (i - 1) * 2 + half + 1)
                    pool.tensor_tensor(gate[:, half:half + 1], ones[:], ones[:], ALU.mult)
                    pool.tensor_scalar(u[:, keys], relus[:, 3, keys], iwp[:, 3:4], TIE * HALF * half,
                                       ALU.mult, ALU.add).then_inc(pool_step, 1)
                    pool.tensor_scalar(relus[:, 2, keys], relus[:, 2, keys], iwp[:, 2:3], 0.0,
                                       ALU.mult, ALU.add).then_inc(pool_step, 1)
                    pool.wait_ge(pool_step, n + 1)
                    pool.tensor_tensor(u[:, keys], u[:, keys], tie[:], ALU.add).then_inc(pool_step, 1)
                    pool.wait_ge(pool_step, n + 3)
                    pool.tensor_tensor(u[:, keys], u[:, keys], relus[:, 2, keys], ALU.add).then_inc(pool_step, 1)
                    pool.wait_ge(weighted, i * 2 + half + 1)
                    pool.wait_ge(pool_step, n + 4)
                    pool.tensor_tensor(u[:, keys], u[:, keys], relus[:, 1, keys], ALU.add).then_inc(u_set, 1)
                    n += 4
                pool.sem_clear(pool_step)

            pool.wait_ge(const_set, 5)
            weigh(0)
            with pool.Fori(1, NT) as i:
                weigh(i)

        @block.vector
        def _(dve):
            steps = [0]

            def step(ins):
                steps[0] += 1
                ins.then_inc(dve_step, 1)
                return steps[0]

            def low(i, c):
                dve.wait_ge(pth_set, i * NKN + c + 1)
                if not isinstance(i, int) or i > 0 or c >= 2:
                    dve.wait_ge(o_done, i * NKN + c - 1)
                dve.tensor_tensor(pTl[:, c % 2, :], pt[:], f32(pTh[:, c % 2, :]), ALU.subtract).then_inc(ptl_set, 1)

            def scores(i, half, sc):
                keys = slice(half * HALF, (half + 1) * HALF)
                if half == 0:
                    dve.wait_ge(iwd_loaded, (i + 1) * 16)
                dve.wait_ge(u_set, i * 2 + half + 1)
                dve.wait_ge(relu_set, i * NU + 6 + half + 1)
                dve.scalar_tensor_tensor(sc[:, keys], relus[:, 0, keys], iwd[:, 0:1], u[:, keys],
                                         ALU.mult, ALU.add).then_inc(s_set, 1)

            def group_best(sc, groups):
                for g in groups:
                    n = step(dve.max(cand[:, g * 8:g * 8 + 8], sc[:, g * GRP:(g + 1) * GRP]))
                return n

            def group_rest(sc):
                for g in range(NGRP):
                    n = step(dve.match_replace(rest[:, g * GRP:(g + 1) * GRP], cand[:, g * 8:g * 8 + 8],
                                               sc[:, g * GRP:(g + 1) * GRP], TAKEN))
                return n

            def threshold_round(r, n):
                dve.wait_ge(dve_step, n)
                n = step(dve.max(best[:], cand[:]))
                dve.wait_ge(dve_step, n)
                if r < TOPK // 8 - 1:
                    n = step(dve.match_replace(cand[:], best[:], cand[:], TAKEN))
                return n

            def select_again(sc):
                n = 0
                for r in range(TOPK // 8):
                    dve.max(redo_best[:], sc[:]).then_inc(redo_step, 1)
                    dve.wait_ge(redo_step, n + 1)
                    dve.match_replace(sc[:], redo_best[:], sc[:], TAKEN).then_inc(redo_step, 1)
                    dve.wait_ge(redo_step, n + 2)
                    n += 2
                dve.tensor_scalar(bias[:], sc[:], TAKEN, NEG, ALU.not_equal, ALU.mult).then_inc(redo_step, 1)
                dve.wait_ge(redo_step, n + 1)
                dve.sem_clear(redo_step)

            def checked(i, sc):
                dve.wait_ge(check_done, i + 1)
                n = step(dve.tensor_scalar(redo[:], op[0:1, KN - 1:KN], ALL_OUT, None, ALU.is_gt))
                dve.wait_ge(dve_step, n)
                again = dve.value_load(redo[0:1, 0:1], min_val=0, max_val=1)
                with dve.If(again != 0):
                    select_again(sc)

            def mask(i, quarters):
                for n in quarters:
                    if n == 0 and (not isinstance(i, int) or i > 0):
                        dve.wait_ge(pt_done, i * NKN)
                    keys = slice(n * KN, (n + 1) * KN)
                    dve.wait_ge(l_done, i * NKN + n + 1)
                    dve.memset(dve_gate[:, n:n + 1], 0.0)
                    dve.tensor_tensor_reduce(out=pr[:, keys], in0=bias[:, keys], in1=lp[:, n % 2, :], scale=SCALE,
                                             scalar=TAKEN, op0=ALU.add, op1=ALU.max,
                                             accum_out=mx[:, n:n + 1]).then_inc(m_set, 1)

            def negative_maximum(i):
                dve.wait_ge(m_set, (i + 1) * NKN)
                dve.tensor_reduce(nm[:], mx[:], AX.X, ALU.max, negate=True).then_inc(nm_set, 1)

            def inverse_sum(i):
                dve.wait_ge(p_set, i + 1)
                return step(dve.reciprocal(rinv[:], rsum[:]))

            def output(i, n):
                dve.wait_ge(x1_loaded, (i + 1) * 16)
                dve.wait_ge(o_done, (i + 1) * NKN)
                if not isinstance(i, int) or i > 0:
                    dve.wait_ge(x2_stored, i * 16)
                dve.wait_ge(dve_step, n)
                dve.scalar_tensor_tensor(x2t[:], op[:, 0:D], rinv[:], x1t[:], ALU.mult, ALU.add).then_inc(x2_set, 1)

            def tile(i, parity, before=2):
                mine, other = sc[:, parity, :], sc[:, 1 - parity, :]
                if before > 1:
                    inverse = inverse_sum(i - 2)
                scores(i, 0, mine)
                if before > 1:
                    output(i - 2, inverse)
                scores(i, 1, mine)
                if before > 0:
                    checked(i - 1, other)
                    mask(i - 1, (0, 1))
                dve.wait_ge(s_set, 2 * i + 2)
                dve.memset(dve_gate[:, NKN:NKN + 1], 0.0)
                group_best(mine, range(0, 8))
                if before > 0:
                    mask(i - 1, (2,))
                group_best(mine, range(8, 13))
                if before > 0:
                    mask(i - 1, (3,))
                n = group_best(mine, range(13, 15))
                if before > 0:
                    negative_maximum(i - 1)
                n = group_best(mine, range(15, NGRP))
                dve.wait_ge(dve_step, n)
                n = group_rest(mine)
                if before > 0:
                    low(i - 1, 0)
                dve.wait_ge(dve_step, n)
                n = step(dve.max(cand[:, NGRP * 8:NCAND], rest[:]))
                if before > 0:
                    low(i - 1, 1)
                for r in range(TOPK // 8):
                    n = threshold_round(r, n)
                    if before > 0 and r in (2, 4):
                        low(i - 1, r // 2 + 1)
                dve.tensor_scalar(bias[:], mine, best[:, 7:8], NEG, ALU.is_lt, ALU.mult).then_inc(bias_set, 1)
                dve.sem_clear(dve_step)
                steps[0] = 0

            tile(0, 0, before=0)
            tile(1, 1, before=1)
            with dve.Fori(1, NT // 2) as pair:
                tile(2 * pair, 0)
                tile(2 * pair + 1, 1)
            output(NT - 2, inverse_sum(NT - 2))
            checked(NT - 1, sc[:, 1, :])
            mask(NT - 1, range(NKN))
            negative_maximum(NT - 1)
            for c in range(NKN):
                low(NT - 1, c)
            output(NT - 1, inverse_sum(NT - 1))


_OUTS = [((BATCH, SEQ, D), "float32")]


def kernel(**inputs):
    import concourse.bacc as _bacc
    from concourse.bass_utils import run_bass_kernel_spmd as _run

    a = {k: np.asarray(v) for k, v in inputs.items()}
    last = E - 1
    w_qkv, b_qkv = a["L0_attn_w_qkv"], a["L0_attn_b_qkv"]
    half = D // 2
    inv_freq = (np.float32(1.0) / np.float32(10000.0) ** (np.arange(half, dtype=np.float32) / np.float32(half)))
    ang = np.arange(SEQ, dtype=np.float32)[None, :] * inv_freq.astype(np.float32)[:, None]
    rotations = np.stack([np.cos(ang), np.sin(ang)], 1).reshape(half, 2, SEQ // GR, GR).transpose(2, 0, 1, 3)
    nc = _bacc.Bacc("TRN2", target_bir_lowering=False, num_devices=1)
    arrays = {}

    def give(name, array):
        array = np.ascontiguousarray(array)
        arrays["in_" + name] = array
        return nc.dram_tensor("in_" + name, array.shape, mybir.dt.from_np(array.dtype), kind="ExternalInput").ap()

    d = Tensors()
    d.x = give("x", a["L0_attn_x"].reshape(ROWS, D))
    d.wqkT = give("wqkT", w_qkv[:2 * D].T)
    d.bqk = give("bqk", b_qkv[:2 * D])
    d.wv = give("wv", w_qkv[2 * D:])
    d.bv = give("bv", b_qkv[2 * D:])
    d.woT = give("woT", a["L0_attn_w_o"].T)
    d.bo = give("bo", a["L0_attn_b_o"])
    d.wiqT = give("wiqT", a["L0_attn_w_iq"].T)
    d.biq = give("biq", a["L0_attn_b_iq"])
    d.wikT = give("wikT", a["L0_attn_w_ik"].T)
    d.bik = give("bik", a["L0_attn_b_ik"])
    d.wiwT = give("wiwT", a["L0_attn_w_iw"].T)
    d.biw = give("biw", a["L0_attn_b_iw"])
    d.wrT = give("wrT", a["L0_ffn_Wr"].T)
    d.w1 = give("w1", a["L0_ffn_W1"][last])
    d.b1 = give("b1", a["L0_ffn_b1"][last])
    d.w2 = give("w2", a["L0_ffn_W2"][last])
    d.b2 = give("b2", a["L0_ffn_b2"][last])
    d.cs_t = give("cs_t", np.tile(rotations, (BATCH, 1, 1, 1)))
    d.out = nc.dram_tensor("out_dram", (ROWS, D), FP32, kind="ExternalOutput").ap()
    macaron_kernel(nc, d)
    r = _run(nc, [arrays], core_ids=[0])
    return r.results[0]["out_dram"].reshape(BATCH, SEQ, D)
```
